# Optimizing a Trainium2 kernel written in Bass

```python
import numpy as np
import jax
import jax.numpy as jnp

def _softmax(x, axis=-1):
    return jax.nn.softmax(x, axis=axis)

def _gelu(x):
    return jax.nn.gelu(x, approximate=True)

def _silu(x):
    return jax.nn.silu(x)

def _sigmoid(x):
    return jax.nn.sigmoid(x)

def _layernorm(x, axis=-1, eps=1e-05):
    m = jnp.mean(x, axis=axis, keepdims=True)
    v = jnp.var(x, axis=axis, keepdims=True)
    return (x - m) / jnp.sqrt(v + eps)

def _scatter_add(tgt, idx, src, axis=0):
    return tgt.at[idx].add(src)

def _segment_sum(src, seg, n):
    return jax.ops.segment_sum(src, seg, n)
kernel_name = 'mk_dlrm_tower_d1_rec_r8_751ce1'

def setup_inputs(seed: int=0):
    np.random.seed(seed)
    _w = jnp.asarray

    def _rec_inputs():
        import jax
        import jax.numpy as jnp
        _tk = jax.random.key(seed)
        dense_ctx = jax.random.normal(jax.random.fold_in(_tk, 190), (512, 16), jnp.float32)
        ids = jnp.stack([jax.random.randint(jax.random.fold_in(_tk, 200 + f), (512,), 0, v, jnp.int32) for f, v in enumerate([12500, 125000, 12500, 12500, 1000, 1000, 125000, 125000, 1000, 1000, 125000, 1250, 1250, 1250, 1250, 12500, 12500, 1250, 125000, 1250, 12500, 1250, 125000, 125000, 1250, 1000, 1000, 1250, 1000, 1250, 1250, 1250, 1000, 1250, 1000, 1000, 1250, 1000, 1000, 1250])], axis=1)
        tbl_0 = 0.05 * jax.random.normal(jax.random.fold_in(_tk, 500 + 0), (12500, 32), jnp.float32)
        tbl_1 = 0.05 * jax.random.normal(jax.random.fold_in(_tk, 500 + 1), (125000, 32), jnp.float32)
        tbl_2 = 0.05 * jax.random.normal(jax.random.fold_in(_tk, 500 + 2), (12500, 32), jnp.float32)
        tbl_3 = 0.05 * jax.random.normal(jax.random.fold_in(_tk, 500 + 3), (12500, 32), jnp.float32)
        tbl_4 = 0.05 * jax.random.normal(jax.random.fold_in(_tk, 500 + 4), (1000, 32), jnp.float32)
        tbl_5 = 0.05 * jax.random.normal(jax.random.fold_in(_tk, 500 + 5), (1000, 32), jnp.float32)
        tbl_6 = 0.05 * jax.random.normal(jax.random.fold_in(_tk, 500 + 6), (125000, 32), jnp.float32)
        tbl_7 = 0.05 * jax.random.normal(jax.random.fold_in(_tk, 500 + 7), (125000, 32), jnp.float32)
        tbl_8 = 0.05 * jax.random.normal(jax.random.fold_in(_tk, 500 + 8), (1000, 32), jnp.float32)
        tbl_9 = 0.05 * jax.random.normal(jax.random.fold_in(_tk, 500 + 9), (1000, 32), jnp.float32)
        tbl_10 = 0.05 * jax.random.normal(jax.random.fold_in(_tk, 500 + 10), (125000, 32), jnp.float32)
        tbl_11 = 0.05 * jax.random.normal(jax.random.fold_in(_tk, 500 + 11), (1250, 32), jnp.float32)
        tbl_12 = 0.05 * jax.random.normal(jax.random.fold_in(_tk, 500 + 12), (1250, 32), jnp.float32)
        tbl_13 = 0.05 * jax.random.normal(jax.random.fold_in(_tk, 500 + 13), (1250, 32), jnp.float32)
        tbl_14 = 0.05 * jax.random.normal(jax.random.fold_in(_tk, 500 + 14), (1250, 32), jnp.float32)
        tbl_15 = 0.05 * jax.random.normal(jax.random.fold_in(_tk, 500 + 15), (12500, 32), jnp.float32)
        tbl_16 = 0.05 * jax.random.normal(jax.random.fold_in(_tk, 500 + 16), (12500, 32), jnp.float32)
        tbl_17 = 0.05 * jax.random.normal(jax.random.fold_in(_tk, 500 + 17), (1250, 32), jnp.float32)
        tbl_18 = 0.05 * jax.random.normal(jax.random.fold_in(_tk, 500 + 18), (125000, 32), jnp.float32)
        tbl_19 = 0.05 * jax.random.normal(jax.random.fold_in(_tk, 500 + 19), (1250, 32), jnp.float32)
        tbl_20 = 0.05 * jax.random.normal(jax.random.fold_in(_tk, 500 + 20), (12500, 32), jnp.float32)
        tbl_21 = 0.05 * jax.random.normal(jax.random.fold_in(_tk, 500 + 21), (1250, 32), jnp.float32)
        tbl_22 = 0.05 * jax.random.normal(jax.random.fold_in(_tk, 500 + 22), (125000, 32), jnp.float32)
        tbl_23 = 0.05 * jax.random.normal(jax.random.fold_in(_tk, 500 + 23), (125000, 32), jnp.float32)
        tbl_24 = 0.05 * jax.random.normal(jax.random.fold_in(_tk, 500 + 24), (1250, 32), jnp.float32)
        tbl_25 = 0.05 * jax.random.normal(jax.random.fold_in(_tk, 500 + 25), (1000, 32), jnp.float32)
        tbl_26 = 0.05 * jax.random.normal(jax.random.fold_in(_tk, 500 + 26), (1000, 32), jnp.float32)
        tbl_27 = 0.05 * jax.random.normal(jax.random.fold_in(_tk, 500 + 27), (1250, 32), jnp.float32)
        tbl_28 = 0.05 * jax.random.normal(jax.random.fold_in(_tk, 500 + 28), (1000, 32), jnp.float32)
        tbl_29 = 0.05 * jax.random.normal(jax.random.fold_in(_tk, 500 + 29), (1250, 32), jnp.float32)
        tbl_30 = 0.05 * jax.random.normal(jax.random.fold_in(_tk, 500 + 30), (1250, 32), jnp.float32)
        tbl_31 = 0.05 * jax.random.normal(jax.random.fold_in(_tk, 500 + 31), (1250, 32), jnp.float32)
        tbl_32 = 0.05 * jax.random.normal(jax.random.fold_in(_tk, 500 + 32), (1000, 32), jnp.float32)
        tbl_33 = 0.05 * jax.random.normal(jax.random.fold_in(_tk, 500 + 33), (1250, 32), jnp.float32)
        tbl_34 = 0.05 * jax.random.normal(jax.random.fold_in(_tk, 500 + 34), (1000, 32), jnp.float32)
        tbl_35 = 0.05 * jax.random.normal(jax.random.fold_in(_tk, 500 + 35), (1000, 32), jnp.float32)
        tbl_36 = 0.05 * jax.random.normal(jax.random.fold_in(_tk, 500 + 36), (1250, 32), jnp.float32)
        tbl_37 = 0.05 * jax.random.normal(jax.random.fold_in(_tk, 500 + 37), (1000, 32), jnp.float32)
        tbl_38 = 0.05 * jax.random.normal(jax.random.fold_in(_tk, 500 + 38), (1000, 32), jnp.float32)
        tbl_39 = 0.05 * jax.random.normal(jax.random.fold_in(_tk, 500 + 39), (1250, 32), jnp.float32)
        _rk = jax.random.fold_in(_tk, 7)
        W_top1 = 0.049029 * jax.random.normal(jax.random.fold_in(_tk, 801), (416, 512), jnp.float32)
        W_top2 = 0.0441942 * jax.random.normal(jax.random.fold_in(_tk, 802), (512, 256), jnp.float32)
        W_top3 = 0.0625 * jax.random.normal(jax.random.fold_in(_tk, 803), (256, 1), jnp.float32)
        b_top1 = jnp.zeros((512,), jnp.float32)
        b_top2 = jnp.zeros((256,), jnp.float32)
        return (dense_ctx, ids, tbl_0, tbl_1, tbl_2, tbl_3, tbl_4, tbl_5, tbl_6, tbl_7, tbl_8, tbl_9, tbl_10, tbl_11, tbl_12, tbl_13, tbl_14, tbl_15, tbl_16, tbl_17, tbl_18, tbl_19, tbl_20, tbl_21, tbl_22, tbl_23, tbl_24, tbl_25, tbl_26, tbl_27, tbl_28, tbl_29, tbl_30, tbl_31, tbl_32, tbl_33, tbl_34, tbl_35, tbl_36, tbl_37, tbl_38, tbl_39, W_top1, b_top1, W_top2, b_top2, W_top3)
    dense_ctx, ids, tbl_0, tbl_1, tbl_2, tbl_3, tbl_4, tbl_5, tbl_6, tbl_7, tbl_8, tbl_9, tbl_10, tbl_11, tbl_12, tbl_13, tbl_14, tbl_15, tbl_16, tbl_17, tbl_18, tbl_19, tbl_20, tbl_21, tbl_22, tbl_23, tbl_24, tbl_25, tbl_26, tbl_27, tbl_28, tbl_29, tbl_30, tbl_31, tbl_32, tbl_33, tbl_34, tbl_35, tbl_36, tbl_37, tbl_38, tbl_39, W_top1, b_top1, W_top2, b_top2, W_top3 = _rec_inputs()

    def _L0_rec_setup():
        import jax, jax.numpy as jnp
        import numpy as np
        B, F0, K = (256, 40, 32)
        CIN_SIZE = [200, 200]

        def _cin(inputs, params):
            Bb, F0_, Kk = inputs.shape
            res = inputs
            outs = []
            for wq, wk, wv, cw in params:
                x0_wk = inputs * wk
                x0_wv = inputs * wv
                xi_wq = res * wq
                phi = jnp.einsum('bfk,bgk->bkfg', x0_wk, xi_wq)
                alpha = jax.nn.softmax(phi, axis=2)
                x = alpha * jnp.transpose(x0_wv, (0, 2, 1))[:, :, :, None]
                x = x.reshape(Bb, Kk, -1)
                out = jnp.einsum('bkc,cj->bjk', x, cw[0])
                outs.append(out)
                res = out
            cat = jnp.concatenate(outs, axis=1)
            return cat.sum(axis=-1)
        key = jax.random.key(seed)
        ks = jax.random.split(key, 1 + 4 * len(CIN_SIZE))
        field_num = [F0] + CIN_SIZE
        d = {'inputs': jax.random.normal(ks[0], (B, F0, K), dtype=jnp.float32)}
        for i in range(len(CIN_SIZE)):
            d[f'wq{i}'] = jax.random.normal(ks[1 + 4 * i], (1, field_num[i], K), dtype=jnp.float32) * 0.05
            d[f'wk{i}'] = jax.random.normal(ks[2 + 4 * i], (1, F0, K), dtype=jnp.float32) * 0.05
            d[f'wv{i}'] = jax.random.normal(ks[3 + 4 * i], (1, F0, K), dtype=jnp.float32) * 0.05
            lim = (6.0 / (F0 * field_num[i] + field_num[i + 1])) ** 0.5
            d[f'cw{i}'] = jax.random.uniform(ks[4 + 4 * i], (1, F0 * field_num[i], field_num[i + 1]), minval=-lim, maxval=lim, dtype=jnp.float32)
        return d
    _L0_rec_all = _L0_rec_setup()
    _L0_rec_in = {k: v for k, v in _L0_rec_all.items() if k in ('wq0', 'wk0', 'wv0', 'cw0', 'wq1', 'wk1', 'wv1', 'cw1')}
    del _L0_rec_all
    return {'dense_ctx': dense_ctx, 'ids': ids, 'tbl_0': tbl_0, 'tbl_1': tbl_1, 'tbl_2': tbl_2, 'tbl_3': tbl_3, 'tbl_4': tbl_4, 'tbl_5': tbl_5, 'tbl_6': tbl_6, 'tbl_7': tbl_7, 'tbl_8': tbl_8, 'tbl_9': tbl_9, 'tbl_10': tbl_10, 'tbl_11': tbl_11, 'tbl_12': tbl_12, 'tbl_13': tbl_13, 'tbl_14': tbl_14, 'tbl_15': tbl_15, 'tbl_16': tbl_16, 'tbl_17': tbl_17, 'tbl_18': tbl_18, 'tbl_19': tbl_19, 'tbl_20': tbl_20, 'tbl_21': tbl_21, 'tbl_22': tbl_22, 'tbl_23': tbl_23, 'tbl_24': tbl_24, 'tbl_25': tbl_25, 'tbl_26': tbl_26, 'tbl_27': tbl_27, 'tbl_28': tbl_28, 'tbl_29': tbl_29, 'tbl_30': tbl_30, 'tbl_31': tbl_31, 'tbl_32': tbl_32, 'tbl_33': tbl_33, 'tbl_34': tbl_34, 'tbl_35': tbl_35, 'tbl_36': tbl_36, 'tbl_37': tbl_37, 'tbl_38': tbl_38, 'tbl_39': tbl_39, 'W_top1': W_top1, 'b_top1': b_top1, 'W_top2': W_top2, 'b_top2': b_top2, 'W_top3': W_top3, 'L0_rec_wq0': _L0_rec_in['wq0'], 'L0_rec_wk0': _L0_rec_in['wk0'], 'L0_rec_wv0': _L0_rec_in['wv0'], 'L0_rec_cw0': _L0_rec_in['cw0'], 'L0_rec_wq1': _L0_rec_in['wq1'], 'L0_rec_wk1': _L0_rec_in['wk1'], 'L0_rec_wv1': _L0_rec_in['wv1'], 'L0_rec_cw1': _L0_rec_in['cw1']}

def reference(dense_ctx, ids, tbl_0, tbl_1, tbl_2, tbl_3, tbl_4, tbl_5, tbl_6, tbl_7, tbl_8, tbl_9, tbl_10, tbl_11, tbl_12, tbl_13, tbl_14, tbl_15, tbl_16, tbl_17, tbl_18, tbl_19, tbl_20, tbl_21, tbl_22, tbl_23, tbl_24, tbl_25, tbl_26, tbl_27, tbl_28, tbl_29, tbl_30, tbl_31, tbl_32, tbl_33, tbl_34, tbl_35, tbl_36, tbl_37, tbl_38, tbl_39, W_top1, b_top1, W_top2, b_top2, W_top3, L0_rec_wq0, L0_rec_wk0, L0_rec_wv0, L0_rec_cw0, L0_rec_wq1, L0_rec_wk1, L0_rec_wv1, L0_rec_cw1):
    import jax
    import jax.numpy as jnp

    def _L0_rec_ref(inputs, wq0, wk0, wv0, cw0, wq1, wk1, wv1, cw1):
        import jax, jax.numpy as jnp
        import numpy as np
        B, F0, K = (256, 40, 32)
        CIN_SIZE = [200, 200]

        def _cin(inputs, params):
            Bb, F0_, Kk = inputs.shape
            res = inputs
            outs = []
            for wq, wk, wv, cw in params:
                x0_wk = inputs * wk
                x0_wv = inputs * wv
                xi_wq = res * wq
                phi = jnp.einsum('bfk,bgk->bkfg', x0_wk, xi_wq)
                alpha = jax.nn.softmax(phi, axis=2)
                x = alpha * jnp.transpose(x0_wv, (0, 2, 1))[:, :, :, None]
                x = x.reshape(Bb, Kk, -1)
                out = jnp.einsum('bkc,cj->bjk', x, cw[0])
                outs.append(out)
                res = out
            cat = jnp.concatenate(outs, axis=1)
            return cat.sum(axis=-1)
        return _cin(inputs, [(wq0, wk0, wv0, cw0), (wq1, wk1, wv1, cw1)])
    e = jnp.stack([tbl_0[ids[:, 0]], tbl_1[ids[:, 1]], tbl_2[ids[:, 2]], tbl_3[ids[:, 3]], tbl_4[ids[:, 4]], tbl_5[ids[:, 5]], tbl_6[ids[:, 6]], tbl_7[ids[:, 7]], tbl_8[ids[:, 8]], tbl_9[ids[:, 9]], tbl_10[ids[:, 10]], tbl_11[ids[:, 11]], tbl_12[ids[:, 12]], tbl_13[ids[:, 13]], tbl_14[ids[:, 14]], tbl_15[ids[:, 15]], tbl_16[ids[:, 16]], tbl_17[ids[:, 17]], tbl_18[ids[:, 18]], tbl_19[ids[:, 19]], tbl_20[ids[:, 20]], tbl_21[ids[:, 21]], tbl_22[ids[:, 22]], tbl_23[ids[:, 23]], tbl_24[ids[:, 24]], tbl_25[ids[:, 25]], tbl_26[ids[:, 26]], tbl_27[ids[:, 27]], tbl_28[ids[:, 28]], tbl_29[ids[:, 29]], tbl_30[ids[:, 30]], tbl_31[ids[:, 31]], tbl_32[ids[:, 32]], tbl_33[ids[:, 33]], tbl_34[ids[:, 34]], tbl_35[ids[:, 35]], tbl_36[ids[:, 36]], tbl_37[ids[:, 37]], tbl_38[ids[:, 38]], tbl_39[ids[:, 39]]], axis=1)
    z = _L0_rec_ref(e, L0_rec_wq0, L0_rec_wk0, L0_rec_wv0, L0_rec_cw0, L0_rec_wq1, L0_rec_wk1, L0_rec_wv1, L0_rec_cw1)
    z = z.reshape(z.shape[0], -1)
    h = jnp.concatenate([z, dense_ctx], axis=1)
    h = jnp.maximum(h @ W_top1 + b_top1, 0.0)
    h = jnp.maximum(h @ W_top2 + b_top2, 0.0)
    y = h @ W_top3
    return y

_drawn_inputs = setup_inputs


def setup_inputs(seed=0):
    import zlib

    import numpy as np

    out = dict(_drawn_inputs(seed))
    spreads = {'b_top1': (0.0, 0.1), 'b_top2': (0.0, 0.1)}
    factors = {'tbl_0': 8.0,
     'tbl_1': 8.0,
     'tbl_2': 8.0,
     'tbl_3': 8.0,
     'tbl_4': 8.0,
     'tbl_5': 8.0,
     'tbl_6': 8.0,
     'tbl_7': 8.0,
     'tbl_8': 8.0,
     'tbl_9': 8.0,
     'tbl_10': 8.0,
     'tbl_11': 8.0,
     'tbl_12': 8.0,
     'tbl_13': 8.0,
     'tbl_14': 8.0,
     'tbl_15': 8.0,
     'tbl_16': 8.0,
     'tbl_17': 8.0,
     'tbl_18': 8.0,
     'tbl_19': 8.0,
     'tbl_20': 8.0,
     'tbl_21': 8.0,
     'tbl_22': 8.0,
     'tbl_23': 8.0,
     'tbl_24': 8.0,
     'tbl_25': 8.0,
     'tbl_26': 8.0,
     'tbl_27': 8.0,
     'tbl_28': 8.0,
     'tbl_29': 8.0,
     'tbl_30': 8.0,
     'tbl_31': 8.0,
     'tbl_32': 8.0,
     'tbl_33': 8.0,
     'tbl_34': 8.0,
     'tbl_35': 8.0,
     'tbl_36': 8.0,
     'tbl_37': 8.0,
     'tbl_38': 8.0,
     'tbl_39': 8.0,
     'L0_rec_wq0': 8.0,
     'L0_rec_wk0': 8.0,
     'L0_rec_wv0': 8.0,
     'L0_rec_cw0': 8.0,
     'L0_rec_wq1': 64.0,
     'L0_rec_wk1': 64.0,
     'L0_rec_wv1': 8.0,
     'L0_rec_cw1': 8.0}
    for name, (base, spread) in spreads.items():
        noise = np.random.default_rng([zlib.crc32(name.encode()), seed]).standard_normal(out[name].shape)
        drawn = base * np.exp(spread * noise) if base else spread * noise
        out[name] = jnp.asarray(drawn.astype(out[name].dtype))
    for name, factor in factors.items():
        out[name] = (out[name] * factor).astype(out[name].dtype)
    return out
```

```python
B, F, K, G1 = 512, 40, 32, 200
DENSE, H1, H2 = 16, 512, 256
P = 128
GROUPS = P // K
BLOCKS = B // P
TILES = B // GROUPS
BLOCK_TILES = P // GROUPS
HALF_TILES = 16
HALVES = TILES // HALF_TILES
HALF_ROWS = HALF_TILES * GROUPS
PAIRS0 = F * F
PAIRS1 = F * G1
CHUNKS = 4
CHUNK_F = F // CHUNKS
TCHUNKS = -(-PAIRS0 // P)
TGROUP = 4
TGROUPS = -(-TCHUNKS // TGROUP)
HG = G1 // 2
WAYS = 5
A0, A1, R0, V0, V1 = range(WAYS)
SLOTS = 2 * BLOCK_TILES + 1
REGION0_F = 32


def build(nc, dram, out):
    from contextlib import ExitStack

    import concourse.bass as bass
    from concourse import mybir

    fp32 = mybir.dt.float32
    ALU = mybir.AluOpType
    ACT = mybir.ActivationFunctionType
    X = mybir.AxisListType.X

    with ExitStack() as ctx:
        def sb(name, shape, dt=fp32):
            return ctx.enter_context(nc.sbuf_tensor(name, shape, dt))

        def bank(name):
            return ctx.enter_context(nc.psum_tensor(name, [P, 512], fp32))

        def sem(name):
            return ctx.enter_context(nc.semaphore(name))

        ident = sb("ident", [P, P])
        group_sel = sb("group_sel", [P, GROUPS])
        fold = sb("fold", [P, HALF_ROWS])
        ids_sb = sb("ids_sb", [P, BLOCKS, F], mybir.dt.int32)
        field_w = sb("field_w", [P, WAYS, F])
        wq1 = sb("wq1", [P, G1])
        cw0 = sb("cw0", [P, TCHUNKS, G1])
        cw1 = sb("cw1", [HG, 2, F, G1])
        rows = sb("rows", [P, F, K])
        emb = sb("emb", [P, SLOTS, F])
        ways = [sb(f"ways{i}", [P, WAYS, F]) for i in range(2)]
        ends = [sb(f"ends{i}", [P, 2, 2]) for i in range(2)]
        x0_pad = sb("x0_pad", [P, TCHUNKS * P])
        x0 = x0_pad[:, 0:PAIRS0].rearrange("p (g f) -> p g f", f=F)
        x0t = sb("x0t", [P, TCHUNKS, P])
        low0 = sb("low0", [P, F])
        sum0 = sb("sum0", [P, F])
        res = sb("res", [P, G1])
        r1 = sb("r1", [P, G1])
        low1 = sb("low1", [P, G1])
        x1 = [sb(f"x1_{i}", [P, F, G1]) for i in range(2)]
        inv1 = sb("inv1", [P, G1])
        vsel = sb("vsel", [P, 1320])
        pooled = sb("pooled", [P, 2, G1])
        pooled_t = sb("pooled_t", [HG, 2, F, GROUPS, HALF_TILES])
        z1 = sb("z1", [P, G1])
        zt = sb("zt", [HG, 4, B])
        b1 = sb("b1", [P, H1 // P])
        b2 = sb("b2", [P, H2 // P])
        w3 = sb("w3", [P, H2 // P])

        spare = x1[0][:, :, :].rearrange("p f g -> p (f g)")
        w1 = spare[0:HG, 0:4 * H1].rearrange("p (c n) -> p c n", c=4)
        w1d = spare[0:DENSE, 4 * H1:5 * H1]
        w2 = spare[:, 5 * H1:5 * H1 + 4 * H2].rearrange("p (c n) -> p c n", c=4)
        at = 5 * H1 + 4 * H2
        h1t = spare[:, at:at + 4 * B].rearrange("p (c n) -> p c n", c=4)
        dense_t = spare[0:DENSE, at + 6 * B:at + 7 * B]
        y_sb = spare[0:1, at + 7 * B:at + 8 * B]
        h2t = spare[:, at + 4 * B:at + 6 * B].rearrange("p (c n) -> p c n", c=2)

        turn = [bank("turn0"), bank("turn1")]
        res_bank = bank("res_bank")
        res_ps = res_bank[:, 0:G1]
        z0_ps = res_bank[0:HG, 256:256 + 2 * GROUPS].rearrange("p (c b) -> p c b", c=2)
        sum1 = [bank(f"sum1_{i}")[:, 0:G1] for i in range(2)]
        small = bank("small")
        top1 = small[:, 0:G1]
        rcp1 = small[:, 208:208 + G1]
        top0 = small[:, 416:416 + F]
        rcp0 = small[:, 464:464 + F]
        pooled_ps = bank("pooled_ps")
        pooled_view = pooled_ps[:, :].rearrange("p (r g) -> p r g", r=2)
        pt_ps = pooled_ps[0:HG, :].rearrange("p (c r q) -> p c r q", c=2, r=2)
        misc = bank("misc")

        loads_in = sem("loads_in")
        cw1_in = sem("cw1_in")
        mlp_in = sem("mlp_in")
        pads_cleared = sem("pads_cleared")
        ident_cleared = sem("ident_cleared")
        ident_ready = sem("ident_ready")
        sel_ready = sem("sel_ready")
        vsel_cleared = sem("vsel_cleared")
        rows_in = sem("rows_in")
        emb_turned = sem("emb_turned")
        emb_ready = sem("emb_ready")
        ways_ready = sem("ways_ready")
        outer_ready = sem("outer_ready")
        ends_ready = sem("ends_ready")
        low0_ready = sem("low0_ready")
        top0_ready = sem("top0_ready")
        shifted0 = sem("shifted0")
        exp0_ready = sem("exp0_ready")
        sum0_ready = sem("sum0_ready")
        rcp0_ready = sem("rcp0_ready")
        norm0_ready = sem("norm0_ready")
        weighed0 = sem("weighed0")
        turned0 = sem("turned0")
        x0t_ready = sem("x0t_ready")
        res_done = sem("res_done")
        res_copied = sem("res_copied")
        z0_summed = sem("z0_summed")
        z0_kept = sem("z0_kept")
        r1_ready = sem("r1_ready")
        low1_ready = sem("low1_ready")
        top1_ready = sem("top1_ready")
        args_ready = sem("args_ready")
        exp1_ready = sem("exp1_ready")
        sum1_done = sem("sum1_done")
        rcp1_ready = sem("rcp1_ready")
        inv1_ready = sem("inv1_ready")
        norm1_v = sem("norm1_v")
        norm1_p = sem("norm1_p")
        vsel_ready = sem("vsel_ready")
        pooled_done = sem("pooled_done")
        pooled_copied = sem("pooled_copied")
        pooled_turned = sem("pooled_turned")
        pooled_kept = sem("pooled_kept")
        z1_done = sem("z1_done")
        z1_copied = sem("z1_copied")
        z1_turned = sem("z1_turned")
        z1_kept = sem("z1_kept")
        h1_done = sem("h1_done")
        h1_ready = sem("h1_ready")
        h2_done = sem("h2_done")
        h2_ready = sem("h2_ready")
        y_done = sem("y_done")
        y_ready = sem("y_ready")
        stored = sem("stored")

        def need(eng, semaphore, count):
            if not isinstance(count, int) or count > 0:
                eng.wait_ge(semaphore, count)

        def tiles(eng, step, between):
            step(-1, 1)
            for half in range(HALVES):
                first = half * HALF_TILES
                step(first, 0)
                between(half)
                step(first + 1, 1)
                pairs = HALF_TILES // 2
                last = pairs - 1 if half < HALVES - 1 else pairs - 1 - 1
                with eng.Fori(1, 1 + last) as i:
                    step(first + 2 * i, 0)
                    step(first + 2 * i + 1, 1)
                if half == HALVES - 1:
                    step(TILES - 2, 0)
                    step(TILES - 1, 1)
            step(TILES, 0)
            between(HALVES)

        def stages(n):
            known = isinstance(n, int)
            return (not known or 0 <= n < TILES, not known or n > 0, not known or n < TILES - 1)

        block = ctx.enter_context(nc.Block())

        @block.sync
        def _(sp):
            sp.dma_start(ids_sb[:, :, :], dram["ids"].rearrange("(t p) f -> p t f", p=P)).then_inc(loads_in, 16)
            for g in range(GROUPS):
                at_g = slice(g * K, (g + 1) * K)
                sp.dma_start(field_w[at_g, :, :], dram["field_w"]).then_inc(loads_in, 16)
                sp.dma_start(wq1[at_g, :], dram["wq1"]).then_inc(loads_in, 16)
            full = PAIRS0 // P
            sp.dma_start(cw0[:, 0:full, :], dram["cw0"][0:full * P, :].rearrange("(c p) j -> p c j", p=P)).then_inc(loads_in, 16)
            sp.dma_start(cw0[0:PAIRS0 - full * P, full, :], dram["cw0"][full * P:PAIRS0, :]).then_inc(loads_in, 16)
            sp.dma_start(b1[:, :], dram["b1"]).then_inc(loads_in, 16)
            sp.dma_start(b2[:, :], dram["b2"]).then_inc(loads_in, 16)
            sp.dma_start(w3[:, :], dram["w3"]).then_inc(loads_in, 16)
            for c in range(2):
                sp.dma_start(cw1[:, c, :, :], dram["cw1"][:, c, :, :]).then_inc(cw1_in, 16)
            sp.wait_ge(pooled_done, CHUNKS * (TILES - 1))
            sp.dma_start(w1, dram["w1"][0:4 * HG, :].rearrange("(c p) n -> p c n", p=HG)).then_inc(mlp_in, 16)
            sp.dma_start(dense_t, dram["dense_t"]).then_inc(mlp_in, 16)
            sp.dma_start(w1d, dram["w1"][4 * HG:4 * HG + DENSE, :]).then_inc(mlp_in, 16)
            sp.dma_start(w2, dram["w2"].rearrange("(c p) n -> p c n", p=P)).then_inc(mlp_in, 16)
            sp.wait_ge(y_ready, 1)
            sp.dma_start(out, y_sb).then_inc(stored, 16)
            sp.wait_ge(stored, 16)
        LOADS = 16 * (1 + 2 * GROUPS + 2 + 3)

        @block.gpsimd
        def _(pool):
            pool.memset(ident[:, :], 0.0).then_inc(ident_cleared, 1)
            pool.wait_ge(ident_cleared, 1)
            pool.affine_select(out=ident[:, :], in_=ident[:, :], compare_op=ALU.not_equal, fill=1.0,
                               base=0, pattern=[[-1, P]], channel_multiplier=1).then_inc(ident_ready, 1)
            pool.memset(x0_pad[:, PAIRS0:], 0.0).then_inc(pads_cleared, 1)
            pool.memset(vsel[:, :], 0.0).then_inc(vsel_cleared, 1)
            pool.wait_ge(loads_in, LOADS)

            def gather(t):
                need(pool, emb_turned, F * t)
                for f in range(F):
                    pool.indirect_dma_start(
                        out=rows[:, f, :], out_offset=None, in_=dram[f"tbl_{f}"],
                        in_offset=bass.IndirectOffsetOnAxis(ap=ids_sb[:, t, f:f + 1], axis=0),
                    ).then_inc(rows_in, 16)

            gather(0)
            pool.wait_ge(sel_ready, 2)
            pool.wait_ge(vsel_cleared, 1)

            def step(n, p):
                here, prev, nxt = stages(n)
                q = 1 - p
                if nxt:
                    if isinstance(n, int):
                        slot = (n + 1) % (2 * BLOCK_TILES)
                        need(pool, emb_ready, 3 * ((n + 1) // BLOCK_TILES + 1))
                        e = emb[:, slot:slot + 1, :]
                    else:
                        e = emb[:, bass.ds(n + 1 - slot_base[0], 1), :]
                    need(pool, args_ready, CHUNKS * n)
                    need(pool, weighed0, n)
                    need(pool, vsel_ready, 2 * n)
                    pool.tensor_tensor(ways[q][:, :, :], e.to_broadcast([P, WAYS, F]), field_w[:, :, :],
                                       ALU.mult).then_inc(ways_ready, 1)
                    pool.wait_ge(ways_ready, n + 2)
                    need(pool, turned0, TGROUPS * (n + 1))
                    pool.tensor_tensor(x0[:, :, :], ways[q][:, A0:A0 + 1, :].to_broadcast([P, F, F]),
                                       ways[q][:, R0, :].unsqueeze(2).to_broadcast([P, F, F]),
                                       ALU.mult).then_inc(outer_ready, 1)
                    pool.wait_ge(norm0_ready, n + 2)
                    pool.tensor_tensor(x0[:, :, :], x0[:, :, :], ways[q][:, V0:V0 + 1, :].to_broadcast([P, F, F]),
                                       ALU.mult).then_inc(weighed0, 1)
                if prev:
                    pool.wait_ge(inv1_ready, n)
                    last = x1[q][:, F - CHUNK_F:F, :]
                    pool.tensor_tensor(last, last, inv1[:, :].unsqueeze(1).to_broadcast([P, CHUNK_F, G1]),
                                       ALU.mult).then_inc(norm1_p, 1)
                if here:
                    need(pool, pooled_done, CHUNKS * n)
                    for lo, count, base in ((0, 8, 0), (8, 2, 8 * P)):
                        pool.tensor_tensor(
                            vsel[:, base:base + 132 * count].rearrange("p (i x) -> p i x", x=132)[:, :, 0:P]
                            .rearrange("p i (j c) -> p i j c", c=32)[:, :, :, 0:GROUPS],
                            ways[p][:, V1, 4 * lo:4 * (lo + count)].rearrange("p (i j) -> p i j", j=4)
                            .unsqueeze(3).to_broadcast([P, count, 4, GROUPS]),
                            group_sel[:, :].unsqueeze(1).unsqueeze(1).to_broadcast([P, count, 4, GROUPS]),
                            ALU.mult).then_inc(vsel_ready, 1)

            slot_base = [0]

            def between(half):
                if half % 2 == 0 and half < HALVES and half // 2 + 1 < BLOCKS:
                    gather(half // 2 + 1)
                if half % 2 and half // 2 + 1 < BLOCKS:
                    pool.wait_ge(emb_ready, 3 * (half // 2 + 2))
                slot_base[0] = half // 4 * 2 * BLOCK_TILES

            tiles(pool, step, between)

        @block.vector
        def _(dve):
            dve.memset(cw0[PAIRS0 % P:P, TCHUNKS - 1, :], 0.0).then_inc(pads_cleared, 1)
            dve.wait_ge(ident_ready, 1)
            dve.tensor_reduce(group_sel[:, :], ident[:, :].rearrange("p (b k) -> p b k", k=K), X, ALU.add).then_inc(sel_ready, 1)
            dve.tensor_tensor(fold[:, :], ident[:, 0:HALF_ROWS], ident[:, HALF_ROWS:P], ALU.add).then_inc(sel_ready, 1)
            dve.wait_ge(loads_in, LOADS)

            def exponents(n, p, c):
                need(dve, pooled_done, CHUNKS * (n - 2) + c + 1)
                for f in range(c * CHUNK_F, (c + 1) * CHUNK_F):
                    last = dve.scalar_tensor_tensor(out=x1[p][:, f, :], in0=r1[:, :], scalar=ways[p][:, A1, f:f + 1],
                                                    in1=top1, op0=ALU.mult, op1=ALU.subtract)
                last.then_inc(args_ready, 1)

            def step(n, p):
                here, prev, nxt = stages(n)
                q = 1 - p
                if here:
                    dve.wait_ge(res_copied, n + 1)
                    need(dve, args_ready, CHUNKS * n)
                    dve.tensor_tensor(r1[:, :], res[:, :], wq1[:, :], ALU.mult).then_inc(r1_ready, 1)
                    dve.wait_ge(r1_ready, n + 1)
                    dve.tensor_scalar(low1[:, :], r1[:, :], ends[p][:, 1, 1:2], None, ALU.mult).then_inc(low1_ready, 1)
                    dve.wait_ge(low1_ready, n + 1)
                    dve.scalar_tensor_tensor(out=top1, in0=r1[:, :], scalar=ends[p][:, 0, 1:2], in1=low1[:, :],
                                             op0=ALU.mult, op1=ALU.max).then_inc(top1_ready, 1)
                    dve.wait_ge(top1_ready, n + 1)
                    exponents(n, p, 0)
                if nxt:
                    dve.wait_ge(ways_ready, n + 2)
                    dve.tensor_reduce(ends[q][:, 0, :], ways[q][:, A0:A1 + 1, :], X, ALU.max).then_inc(ends_ready, 1)
                    dve.tensor_reduce(ends[q][:, 1, :], ways[q][:, A0:A1 + 1, :], X, ALU.min).then_inc(ends_ready, 1)
                    dve.wait_ge(ends_ready, 2 * (n + 2))
                    dve.tensor_scalar(low0[:, :], ways[q][:, R0, :], ends[q][:, 1, 0:1], None, ALU.mult).then_inc(low0_ready, 1)
                    dve.wait_ge(low0_ready, n + 2)
                    dve.scalar_tensor_tensor(out=top0, in0=ways[q][:, R0, :], scalar=ends[q][:, 0, 0:1], in1=low0[:, :],
                                             op0=ALU.mult, op1=ALU.max).then_inc(top0_ready, 1)
                    dve.wait_ge(top0_ready, n + 2)
                    dve.wait_ge(outer_ready, n + 2)
                    dve.tensor_tensor(x0[:, :, :], x0[:, :, :], top0.unsqueeze(2).to_broadcast([P, F, F]),
                                      ALU.subtract).then_inc(shifted0, 1)
                if here:
                    exponents(n, p, 1)
                if nxt:
                    dve.wait_ge(exp0_ready, n + 2)
                    dve.tensor_reduce(sum0[:, :], x0[:, :, :], X, ALU.add).then_inc(sum0_ready, 1)
                    dve.wait_ge(sum0_ready, n + 2)
                    dve.reciprocal(rcp0, sum0[:, :]).then_inc(rcp0_ready, 1)
                    dve.wait_ge(rcp0_ready, n + 2)
                    dve.tensor_tensor(x0[:, :, :], x0[:, :, :], rcp0.unsqueeze(2).to_broadcast([P, F, F]),
                                      ALU.mult).then_inc(norm0_ready, 1)
                if prev:
                    dve.wait_ge(sum1_done, n)
                    need(dve, norm1_p, n - 1)
                    dve.reciprocal(inv1[:, :], sum1[q]).then_inc(inv1_ready, 1)
                    dve.wait_ge(inv1_ready, n)
                    dve.tensor_copy(rcp1, inv1[:, :]).then_inc(rcp1_ready, 1)
                    dve.wait_ge(rcp1_ready, n)
                    for c in range(CHUNKS - 1):
                        part = x1[q][:, c * CHUNK_F:(c + 1) * CHUNK_F, :]
                        dve.tensor_tensor(part, part, rcp1.unsqueeze(1).to_broadcast([P, CHUNK_F, G1]),
                                          ALU.mult).then_inc(norm1_v, 1)
                if here:
                    exponents(n, p, 2)
                    exponents(n, p, 3)

            tiles(dve, step, lambda half: None)

        @block.scalar
        def _(act):
            act.wait_ge(loads_in, LOADS)

            def keep_rows(t):
                for r, lo in enumerate(range(0, F, 16)):
                    hi = min(lo + 16, F)
                    act.wait_ge(emb_turned, F * t + hi)
                    src = misc[:, 0:(hi - lo) * BLOCK_TILES].rearrange("p (f t) -> p t f", t=BLOCK_TILES)
                    base = t % 2 * BLOCK_TILES
                    if t == 2:
                        act.copy(emb[:, SLOTS - 1, lo:hi], src[:, 0, :])
                    act.copy(emb[:, base:base + BLOCK_TILES, lo:hi], src).then_inc(emb_ready, 1)

            keep_rows(0)

            def exp1(n, p, c):
                act.wait_ge(args_ready, CHUNKS * n + c + 1)
                part = x1[p][:, c * CHUNK_F:(c + 1) * CHUNK_F, :]
                act.activation(part, part, ACT.Exp).then_inc(exp1_ready, 1)

            half_of = [0]

            def step(n, p):
                here, prev, nxt = stages(n)
                q = 1 - p
                if here:
                    exp1(n, p, 0)
                if nxt:
                    act.wait_ge(shifted0, n + 2)
                    act.activation(x0[:, :, :], x0[:, :, :], ACT.Exp).then_inc(exp0_ready, 1)
                if here:
                    exp1(n, p, 1)
                if nxt:
                    need(act, res_done, n + 1)
                    for g in range(TGROUPS):
                        act.wait_ge(turned0, TGROUPS * (n + 1) + g + 1)
                        lo, hi = TGROUP * g, min(TGROUP * (g + 1), TCHUNKS)
                        act.copy(x0t[:, lo:hi, :], turn[g % 2][:, 0:(hi - lo) * P].rearrange("p (c q) -> p c q", q=P)
                                 ).then_inc(x0t_ready, 1)
                    act.wait_ge(res_done, n + 2)
                    need(act, z0_summed, n + 1)
                    need(act, r1_ready, n + 1)
                    act.copy(res[:, :], res_ps).then_inc(res_copied, 1)
                    act.wait_ge(z0_summed, n + 2)
                    act.copy(zt[:, 0:2, bass.ds(GROUPS * (n + 1), GROUPS)], z0_ps).then_inc(z0_kept, 1)
                if here:
                    exp1(n, p, 2)
                if prev:
                    act.wait_ge(pooled_done, CHUNKS * n)
                    need(act, pooled_turned, n - 1)
                    act.copy(pooled[:, :, :], pooled_view[:, :, 0:G1]).then_inc(pooled_copied, 1)
                    act.wait_ge(pooled_turned, n)
                    if isinstance(n, int):
                        t = (n - 1) % HALF_TILES
                        need(act, z1_done, (n - 1) // HALF_TILES)
                        spot = lambda v: v[:, :, :, t]
                    else:
                        spot = lambda v: v[:, :, :, bass.ds(n - 1 - half_of[0] * HALF_TILES, 1)].rearrange("p c q o -> p c (q o)")
                    flat = pooled_t[:, :, :, :, :].rearrange("p c f b t -> p c (f b) t")
                    act.copy(spot(flat[:, :, 0:REGION0_F * GROUPS, :]), pt_ps[:, :, 0, :]).then_inc(pooled_kept, 1)
                    v = spot(flat[:, :, REGION0_F * GROUPS:F * GROUPS, :]).rearrange("p c (j x) -> p c j x", j=4)
                    act.copy(v, pt_ps[:, :, 1, :].rearrange("p c (j x) -> p c j x", j=4)[:, :, :, 0:8]).then_inc(pooled_kept, 1)
                if here:
                    exp1(n, p, 3)

            def between(half):
                if half:
                    act.wait_ge(z1_done, half)
                    need(act, z1_turned, half - 1)
                    act.copy(z1[:, :], misc[:, 0:G1]).then_inc(z1_copied, 1)
                    act.wait_ge(z1_turned, half)
                    dst = zt[:, 2:4, (half - 1) * HALF_ROWS:half * HALF_ROWS].rearrange("p c (t b) -> p c b t", b=GROUPS)
                    for c in range(2):
                        act.copy(dst[:, c], misc[0:HG, 256 + HALF_ROWS * c:256 + HALF_ROWS * (c + 1)]
                                 .rearrange("p (b t) -> p b t", t=HALF_TILES)).then_inc(z1_kept, 1)
                if half < HALVES and half % 2 and half // 2 + 1 < BLOCKS:
                    keep_rows(half // 2 + 1)
                half_of[0] = half

            tiles(act, step, between)

            for m in range(H1 // P):
                act.wait_ge(h1_done, m + 1)
                act.activation(h1t[:, m, :], turn[m % 2][:, :], ACT.Relu, bias=b1[:, m:m + 1]).then_inc(h1_ready, 1)
            for m in range(H2 // P):
                act.wait_ge(h2_done, m + 1)
                act.activation(h2t[:, m, :], turn[m % 2][:, :], ACT.Relu, bias=b2[:, m:m + 1]).then_inc(h2_ready, 1)
            act.wait_ge(y_done, 1)
            act.copy(y_sb.rearrange("o (x g t) -> o x t g", g=GROUPS, t=BLOCK_TILES),
                     res_bank[0:1, :].rearrange("o (x t g) -> o x t g", g=GROUPS, t=BLOCK_TILES)).then_inc(y_ready, 1)

        @block.tensor
        def _(pe):
            pe.wait_ge(ident_ready, 1)
            pe.wait_ge(pads_cleared, 2)
            pe.wait_ge(sel_ready, 2)
            pe.wait_ge(loads_in, LOADS)

            def turn_rows(t):
                for f in range(F):
                    if f == 0:
                        pe.wait_ge(rows_in, 16 * F * (t + 1))
                    if f % 16 == 0:
                        need(pe, emb_ready, 3 * t + f // 16)
                        if t and f == 0:
                            pe.wait_ge(z1_kept, 2 * (2 * t - 1))
                    at_f = slice(f % 16 * BLOCK_TILES, (f % 16 + 1) * BLOCK_TILES)
                    for g in range(GROUPS):
                        at_g = slice(g * K, (g + 1) * K)
                        last = pe.matmul(misc[at_g, at_f], rows[:, f, :],
                                         ident[:, at_g], start=True, stop=True)
                    last.then_inc(emb_turned, 1)

            turn_rows(0)

            def sums(n, p, c):
                pe.wait_ge(exp1_ready, CHUNKS * n + c + 1)
                if c == 0:
                    need(pe, inv1_ready, n - 1)
                for f in range(c * CHUNK_F, (c + 1) * CHUNK_F):
                    last = pe.matmul(sum1[p], ident[:, :], x1[p][:, f, :], start=f == 0, stop=f == F - 1)
                if c == CHUNKS - 1:
                    last.then_inc(sum1_done, 1)

            def turn0(n, g):
                if g == 0:
                    pe.wait_ge(weighed0, n + 1)
                need(pe, x0t_ready, TGROUPS * n + g - 1)
                for c in range(TGROUP * g, min(TGROUP * (g + 1), TCHUNKS)):
                    last = pe.transpose(turn[g % 2][:, (c % TGROUP) * P:(c % TGROUP + 1) * P],
                                        x0_pad[:, c * P:(c + 1) * P], ident[:, :])
                last.then_inc(turned0, 1)

            def pool_k(n, q, c):
                if c < CHUNKS - 1:
                    pe.wait_ge(norm1_v, (CHUNKS - 1) * n + c + 1)
                else:
                    pe.wait_ge(norm1_p, n + 1)
                if c == 0:
                    pe.wait_ge(vsel_ready, 2 * (n + 1))
                    need(pe, pooled_kept, 2 * n)
                for f in range(c * CHUNK_F, (c + 1) * CHUNK_F):
                    j, region = f % 4, f // REGION0_F
                    i, count = (f - REGION0_F * region) // 4, (REGION0_F, F - REGION0_F)[region] // 4
                    last = pe.matmul(pooled_ps[32 * j:32 * (j + 1), 256 * region:256 * region + G1],
                                     vsel[:, 32 * f:32 * (f + 1)], x1[q][:, f, :],
                                     start=i == 0, stop=i == count - 1)
                last.then_inc(pooled_done, 1)

            def step(n, p):
                here, prev, nxt = stages(n)
                q = 1 - p
                if here:
                    sums(n, p, 0)
                    sums(n, p, 1)
                if nxt:
                    turn0(n + 1, 0)
                    turn0(n + 1, 1)
                if prev:
                    pool_k(n - 1, q, 0)
                if nxt:
                    turn0(n + 1, 2)
                    turn0(n + 1, 3)
                if prev:
                    pool_k(n - 1, q, 1)
                if nxt:
                    need(pe, z0_kept, n + 1)
                    for c in range(TCHUNKS):
                        if c % TGROUP == 0:
                            pe.wait_ge(x0t_ready, TGROUPS * (n + 1) + c // TGROUP + 1)
                        last = pe.matmul(res_ps, x0t[:, c, :], cw0[:, c, :], start=c == 0, stop=c == TCHUNKS - 1)
                    last.then_inc(res_done, 1)
                if prev:
                    pool_k(n - 1, q, 2)
                if nxt:
                    pe.wait_ge(res_copied, n + 2)
                    for c in range(2):
                        last = pe.matmul(z0_ps[:, c, :], res[:, c * HG:(c + 1) * HG], group_sel[:, :], start=True, stop=True)
                    last.then_inc(z0_summed, 1)
                if prev:
                    pool_k(n - 1, q, 3)
                if here:
                    sums(n, p, 2)
                if prev:
                    pe.wait_ge(pooled_copied, n)
                    for c in range(2):
                        for r in range(2):
                            last = pe.transpose(pt_ps[:, c, r, :], pooled[:, r, c * HG:(c + 1) * HG], ident[:, :])
                    last.then_inc(pooled_turned, 1)
                if here:
                    sums(n, p, 3)

            def layer1_product(half):
                if half == 1:
                    pe.wait_ge(cw1_in, 32)
                pe.wait_ge(pooled_kept, 2 * HALF_TILES * half)
                need(pe, z1_kept, 2 * (half - 1))
                pe.wait_ge(emb_ready, 3 * min(BLOCKS, 1 + half // 2))
                flat = pooled_t[:, :, :, :, :].rearrange("p c f b t -> p c f (b t)")
                for c in range(2):
                    for slot in range(F):
                        if slot < REGION0_F:
                            f = slot // 8 + 4 * (slot % 8)
                        else:
                            f = REGION0_F + (slot - REGION0_F) // 2 + 4 * (slot % 2)
                        side = slot % 2
                        last = pe.matmul(misc[HALF_ROWS * side:HALF_ROWS * (side + 1), 0:G1], flat[:, c, slot, :],
                                         cw1[:, c, f, :], start=c == 0 and slot < 2, stop=c == 1 and slot >= F - 2)
                last.then_inc(z1_done, 1)
                pe.wait_ge(z1_copied, half)
                for c in range(2):
                    last = pe.matmul(misc[0:HG, 256 + HALF_ROWS * c:256 + HALF_ROWS * (c + 1)],
                                     z1[:, c * HG:(c + 1) * HG], fold[:, :], start=True, stop=True)
                last.then_inc(z1_turned, 1)

            def between(half):
                if half:
                    layer1_product(half)
                if half < HALVES and half % 2 and half // 2 + 1 < BLOCKS:
                    turn_rows(half // 2 + 1)

            tiles(pe, step, between)

            pe.wait_ge(mlp_in, 64)
            pe.wait_ge(z1_kept, 2 * HALVES)
            pe.wait_ge(z0_kept, TILES)
            for m in range(H1 // P):
                need(pe, h1_ready, m - 1)
                cols = slice(m * P, (m + 1) * P)
                for c in range(4):
                    pe.matmul(turn[m % 2][:, :], w1[:, c, cols], zt[:, c, :], start=c == 0, stop=False)
                pe.matmul(turn[m % 2][:, :], w1d[:, cols], dense_t, start=False, stop=True).then_inc(h1_done, 1)
            pe.wait_ge(h1_ready, H1 // P)
            for m in range(H2 // P):
                for c in range(H1 // P):
                    last = pe.matmul(turn[m % 2][:, :], w2[:, c, m * P:(m + 1) * P], h1t[:, c, :],
                                     start=c == 0, stop=c == H1 // P - 1)
                last.then_inc(h2_done, 1)
            pe.wait_ge(h2_ready, H2 // P)
            for c in range(H2 // P):
                last = pe.matmul(res_bank[0:1, :], w3[:, c:c + 1], h2t[:, c, :], start=c == 0, stop=c == H2 // P - 1)
            last.then_inc(y_done, 1)


def kernel(**inputs):
    import numpy as np
    import concourse.bacc as bacc
    from concourse import mybir
    from concourse.bass_utils import run_bass_kernel_spmd

    a = {k: np.asarray(v) for k, v in inputs.items()}
    by_k = lambda name: a[name][0].T
    laid = {
        "ids": a["ids"],
        "field_w": np.stack([by_k(f"L0_rec_{w}") for w in ("wk0", "wk1", "wq0", "wv0", "wv1")], axis=1),
        "wq1": by_k("L0_rec_wq1"),
        "cw0": a["L0_rec_cw0"][0].reshape(F, F, G1).transpose(1, 0, 2).reshape(PAIRS0, G1),
        "cw1": a["L0_rec_cw1"][0].reshape(F, 2, HG, G1).transpose(2, 1, 0, 3),
        "dense_t": a["dense_ctx"].reshape(BLOCKS, GROUPS, BLOCK_TILES, DENSE).transpose(3, 0, 2, 1).reshape(DENSE, B),
        "w1": a["W_top1"],
        "b1": a["b_top1"].reshape(H1 // P, P).T,
        "w2": a["W_top2"],
        "b2": a["b_top2"].reshape(H2 // P, P).T,
        "w3": a["W_top3"].reshape(H2 // P, P).T,
    }
    for f in range(F):
        laid[f"tbl_{f}"] = a[f"tbl_{f}"]
    laid = {k: np.ascontiguousarray(v) for k, v in laid.items()}

    nc = bacc.Bacc("TRN2", target_bir_lowering=False, num_devices=1)
    dram = {k: nc.dram_tensor(f"in_{k}", v.shape, mybir.dt.from_np(v.dtype), kind="ExternalInput").ap() for k, v in laid.items()}
    out = nc.dram_tensor("out", (B, 1), mybir.dt.float32, kind="ExternalOutput").ap()
    build(nc, dram, out.rearrange("b o -> o b"))
    r = run_bass_kernel_spmd(nc, [{f"in_{k}": v for k, v in laid.items()}], core_ids=[0])
    return r.results[0]["out"]
```

```python
B, F, K, G1 = 512, 40, 32, 200
DENSE, H1, H2 = 16, 512, 256
P = 128
GROUPS = P // K
BLOCKS = B // P
TILES = B // GROUPS
BLOCK_TILES = P // GROUPS
HALF_TILES = 16
HALVES = TILES // HALF_TILES
HALF_ROWS = HALF_TILES * GROUPS
PAIRS0 = F * F
CHUNKS = 4
CHUNK_F = F // CHUNKS
SCALED = (3, 8, 8, 8)
SUM_PE = 36
PIECES = (0, 8, 16, 24, 32, 40)
NP = len(PIECES) - 1
V_PIECE = 1
FREED = tuple(next(i for i in range(NP) if PIECES[i + 1] >= (c + 1) * CHUNK_F) + 1 for c in range(CHUNKS))
TCHUNKS = -(-PAIRS0 // P)
TGROUP = 4
TGROUPS = -(-TCHUNKS // TGROUP)
HG = G1 // 2
WAYS = 6
FRONT_WAYS = 4
A0, A1, R0, V0 = range(FRONT_WAYS)
A, V = range(WAYS - FRONT_WAYS)
AHEAD = 2
RING = 2 * BLOCK_TILES
REGION0_F = 32
ROUND_F = 16
ROUNDS = -(-F // ROUND_F)


def build(nc, dram, out):
    from contextlib import ExitStack

    import concourse.bass as bass
    from concourse import mybir

    fp32 = mybir.dt.float32
    ALU = mybir.AluOpType
    ACT = mybir.ActivationFunctionType
    X = mybir.AxisListType.X

    with ExitStack() as ctx:
        def sb(name, shape, dt=fp32):
            return ctx.enter_context(nc.sbuf_tensor(name, shape, dt))

        def bank(name):
            return ctx.enter_context(nc.psum_tensor(name, [P, 512], fp32))

        def sem(name):
            return ctx.enter_context(nc.semaphore(name))

        ident = sb("ident", [P, P])
        group_sel = sb("group_sel", [P, GROUPS])
        fold = sb("fold", [P, HALF_ROWS])
        ids_sb = sb("ids_sb", [P, BLOCKS, F], mybir.dt.int32)
        field_w = sb("field_w", [P, WAYS, F])
        wq1 = sb("wq1", [P, G1])
        idle = sb("idle", [P, 1])
        cw0 = sb("cw0", [P, TCHUNKS, G1])
        cw1 = sb("cw1", [HG, 2, F, G1])
        rows = sb("rows", [P, F, K])
        emb = sb("emb", [P, RING + AHEAD, F])
        ways0 = [sb(f"ways0_{i}", [P, FRONT_WAYS, F]) for i in range(2)]
        ways1 = [sb(f"ways1_{i}", [P, WAYS - FRONT_WAYS, F]) for i in range(2)]
        ends = [sb(f"ends{i}", [P, 2, 2]) for i in range(2)]
        x0_pad = sb("x0_pad", [P, TCHUNKS * P])
        x0 = x0_pad[:, 0:PAIRS0].rearrange("p (g f) -> p g f", f=F)
        x0t = sb("x0t", [P, TCHUNKS, P])
        low0 = sb("low0", [P, F])
        sum0 = sb("sum0", [P, F])
        res = sb("res", [P, G1])
        r1 = sb("r1", [P, G1])
        low1 = sb("low1", [P, G1])
        part1 = low1
        x1 = [sb(f"x1_{i}", [P, F, G1]) for i in range(2)]
        inv1 = sb("inv1", [P, G1])
        vsel = sb("vsel", [P, 1288])
        pooled = sb("pooled", [P, 2, G1])
        pooled_t = sb("pooled_t", [HG, 2, F, GROUPS, HALF_TILES])
        z1 = sb("z1", [P, G1])
        zt = sb("zt", [HG, 4, B])
        b1 = sb("b1", [P, H1 // P])
        b2 = sb("b2", [P, H2 // P])
        w3 = sb("w3", [P, H2 // P])

        spare = x1[0][:, :, :].rearrange("p f g -> p (f g)")
        w1 = spare[0:HG, 0:4 * H1].rearrange("p (c n) -> p c n", c=4)
        w1d = spare[0:DENSE, 4 * H1:5 * H1]
        w2 = spare[:, 5 * H1:5 * H1 + 4 * H2].rearrange("p (c n) -> p c n", c=4)
        at = 5 * H1 + 4 * H2
        h1t = spare[:, at:at + 4 * B].rearrange("p (c n) -> p c n", c=4)
        dense_t = spare[0:DENSE, at + 6 * B:at + 7 * B]
        y_sb = spare[0:1, at + 7 * B:at + 8 * B]
        h2t = spare[:, at + 4 * B:at + 6 * B].rearrange("p (c n) -> p c n", c=2)

        turn = [bank("turn0"), bank("turn1")]
        res_bank = bank("res_bank")
        res_ps = res_bank[:, 0:G1]
        z0_ps = res_bank[0:HG, 256:256 + 2 * GROUPS].rearrange("p (c b) -> p c b", c=2)
        sum1 = [bank(f"sum1_{i}")[:, 0:G1] for i in range(2)]
        small = bank("small")
        top1 = small[:, 0:G1]
        top0 = small[:, 416:416 + F]
        rcp0 = small[:, 464:464 + F]
        pooled_ps = bank("pooled_ps")
        pooled_view = pooled_ps[:, :].rearrange("p (r g) -> p r g", r=2)
        pt_ps = pooled_ps[0:HG, :].rearrange("p (c r q) -> p c r q", c=2, r=2)
        misc = bank("misc")

        loads_in = sem("loads_in")
        cw1_in = sem("cw1_in")
        mlp_in = sem("mlp_in")
        pads_cleared = sem("pads_cleared")
        ident_cleared = sem("ident_cleared")
        ident_ready = sem("ident_ready")
        sel_ready = sem("sel_ready")
        vsel_cleared = sem("vsel_cleared")
        rows_in = [sem(f"rows_in{i}") for i in range(ROUNDS)]
        emb_turned = sem("emb_turned")
        emb_ready = sem("emb_ready")
        ways0_ready = sem("ways0_ready")
        ways1_ready = sem("ways1_ready")
        scaled_ready = sem("scaled_ready")
        part1_ready = sem("part1_ready")
        total1_ready = sem("total1_ready")
        outer_ready = sem("outer_ready")
        ends_ready = sem("ends_ready")
        low0_ready = sem("low0_ready")
        top0_ready = sem("top0_ready")
        shifted0 = sem("shifted0")
        exp0_ready = sem("exp0_ready")
        sum0_ready = sem("sum0_ready")
        rcp0_ready = sem("rcp0_ready")
        norm0_ready = sem("norm0_ready")
        weighed0 = sem("weighed0")
        turned0 = sem("turned0")
        x0t_ready = sem("x0t_ready")
        res_done = sem("res_done")
        res_copied = sem("res_copied")
        z0_summed = sem("z0_summed")
        z0_kept = sem("z0_kept")
        r1_ready = sem("r1_ready")
        low1_ready = sem("low1_ready")
        top1_ready = sem("top1_ready")
        args_ready = sem("args_ready")
        exp1_ready = sem("exp1_ready")
        sum1_done = sem("sum1_done")
        inv1_ready = sem("inv1_ready")
        norm1_v = sem("norm1_v")
        norm1_p = sem("norm1_p")
        vsel_ready = sem("vsel_ready")
        pooled_done = sem("pooled_done")
        pooled_copied = sem("pooled_copied")
        pooled_turned = sem("pooled_turned")
        pooled_kept = sem("pooled_kept")
        z1_done = sem("z1_done")
        z1_copied = sem("z1_copied")
        z1_turned = sem("z1_turned")
        z1_kept = sem("z1_kept")
        h1_done = sem("h1_done")
        h1_ready = sem("h1_ready")
        h2_done = sem("h2_done")
        h2_ready = sem("h2_ready")
        y_done = sem("y_done")
        y_ready = sem("y_ready")
        stored = sem("stored")

        def need(eng, semaphore, count):
            if not isinstance(count, int) or count > 0:
                eng.wait_ge(semaphore, count)

        def tiles(eng, step, once):
            for n in range(-AHEAD, 0):
                step(n, n % 2)
            for half in range(HALVES):
                first = half * HALF_TILES
                step(first, 0)
                once(half, 0)
                step(first + 1, 1)
                once(half, 1)
                pairs = HALF_TILES // 2
                peeled = half == HALVES - 1
                with eng.Fori(1, pairs - peeled) as i:
                    step(first + 2 * i, 0)
                    step(first + 2 * i + 1, 1)
            step(TILES - 2, 0)
            step(TILES - 1, 1)
            step(TILES, 0)
            once(HALVES, 0)
            step(TILES + 1, 1)
            once(HALVES, 1)

        def stages(n):
            known = isinstance(n, int)
            return [not known or 0 <= n + ahead < TILES for ahead in (0, -1, -2, 1, 2)]

        def slot_of(m, half):
            return m % RING if isinstance(m, int) else m - half // 4 * RING

        block = ctx.enter_context(nc.Block())

        @block.sync
        def _(sp):
            sp.dma_start(ids_sb[:, :, :], dram["ids"].rearrange("(t p) f -> p t f", p=P)).then_inc(loads_in, 16)
            for g in range(GROUPS):
                at_g = slice(g * K, (g + 1) * K)
                sp.dma_start(field_w[at_g, :, :], dram["field_w"]).then_inc(loads_in, 16)
                sp.dma_start(wq1[at_g, :], dram["wq1"]).then_inc(loads_in, 16)
            full = PAIRS0 // P
            sp.dma_start(cw0[:, 0:full, :], dram["cw0"][0:full * P, :].rearrange("(c p) j -> p c j", p=P)).then_inc(loads_in, 16)
            sp.dma_start(cw0[0:PAIRS0 - full * P, full, :], dram["cw0"][full * P:PAIRS0, :]).then_inc(loads_in, 16)
            sp.dma_start(b1[:, :], dram["b1"]).then_inc(loads_in, 16)
            sp.dma_start(b2[:, :], dram["b2"]).then_inc(loads_in, 16)
            sp.dma_start(w3[:, :], dram["w3"]).then_inc(loads_in, 16)
            for c in range(2):
                sp.dma_start(cw1[:, c, :, :], dram["cw1"][:, c, :, :]).then_inc(cw1_in, 16)
            sp.wait_ge(pooled_done, NP * (TILES - 1))
            sp.dma_start(w1, dram["w1"][0:4 * HG, :].rearrange("(c p) n -> p c n", p=HG)).then_inc(mlp_in, 16)
            sp.dma_start(dense_t, dram["dense_t"]).then_inc(mlp_in, 16)
            sp.dma_start(w1d, dram["w1"][4 * HG:4 * HG + DENSE, :]).then_inc(mlp_in, 16)
            sp.dma_start(w2, dram["w2"].rearrange("(c p) n -> p c n", p=P)).then_inc(mlp_in, 16)
            sp.wait_ge(y_ready, 1)
            sp.dma_start(out, y_sb).then_inc(stored, 16)
            sp.wait_ge(stored, 16)
        LOADS = 16 * (1 + 2 * GROUPS + 2 + 3)

        @block.gpsimd
        def _(pool):
            pool.memset(ident[:, :], 0.0).then_inc(ident_cleared, 1)
            pool.wait_ge(ident_cleared, 1)
            pool.affine_select(out=ident[:, :], in_=ident[:, :], compare_op=ALU.not_equal, fill=1.0,
                               base=0, pattern=[[-1, P]], channel_multiplier=1).then_inc(ident_ready, 1)
            pool.memset(x0_pad[:, PAIRS0:], 0.0).then_inc(pads_cleared, 1)
            pool.memset(vsel[:, :], 0.0).then_inc(vsel_cleared, 1)
            pool.wait_ge(loads_in, LOADS)

            def gather(t, lo, hi):
                need(pool, emb_turned, F * t)
                for f in range(lo, hi):
                    pool.indirect_dma_start(
                        out=rows[:, f, :], out_offset=None, in_=dram[f"tbl_{f}"],
                        in_offset=bass.IndirectOffsetOnAxis(ap=ids_sb[:, t, f:f + 1], axis=0),
                    ).then_inc(rows_in[f // ROUND_F], 16)

            gather(0, 0, F)
            pool.wait_ge(sel_ready, 2)
            pool.wait_ge(vsel_cleared, 1)
            now = [0]

            def normalise(n, q, i):
                part = x1[q][:, PIECES[i]:PIECES[i + 1], :]
                pool.tensor_tensor(part, part, inv1[:, :].unsqueeze(1).to_broadcast([P, PIECES[i + 1] - PIECES[i], G1]),
                                   ALU.mult).then_inc(norm1_p, 1)

            def times_e(dst, m, ways):
                at = slot_of(m, now[0])
                count = ways.stop - ways.start
                return pool.tensor_tensor(dst, emb[:, bass.ds(at, 1), :].to_broadcast([P, count, F]),
                                          field_w[:, ways, :], ALU.mult)

            def step(n, p):
                here, prev, done, back, front = stages(n)
                q = 1 - p
                if back:
                    need(pool, args_ready, CHUNKS * n)
                if front:
                    need(pool, weighed0, n + 1)
                    need(pool, ends_ready, 2 * (n + 1))
                    need(pool, top0_ready, n + 1)
                if prev:
                    need(pool, pooled_done, NP * (n - 1))
                    for lo, count, base in ((0, 8, 0), (8, 2, 8 * P)):
                        pool.tensor_tensor(
                            vsel[:, base:base + 132 * count].rearrange("p (i x) -> p i x", x=132)[:, :, 0:P]
                            .rearrange("p i (j c) -> p i j c", c=32)[:, :, :, 0:GROUPS],
                            ways1[q][:, V, 4 * lo:4 * (lo + count)].rearrange("p (i j) -> p i j", j=4)
                            .unsqueeze(3).to_broadcast([P, count, 4, GROUPS]),
                            group_sel[:, :].unsqueeze(1).unsqueeze(1).to_broadcast([P, count, 4, GROUPS]),
                            ALU.mult).then_inc(vsel_ready, 1)
                if isinstance(n, int) and (front or back):
                    newest = min(n + AHEAD, TILES - 1) // BLOCK_TILES
                    pool.wait_ge(emb_ready, ROUNDS * (newest + 1))
                if front:
                    times_e(ways0[p][:, :, :], n + 2, slice(0, FRONT_WAYS)).then_inc(ways0_ready, 1)
                if back:
                    need(pool, vsel_ready, 2 * n)
                if front:
                    pool.wait_ge(ways0_ready, n + 3)
                    need(pool, turned0, TGROUPS * (n + 2))
                    pool.tensor_tensor(x0, ways0[p][:, A0:A0 + 1, :].to_broadcast([P, F, F]),
                                       ways0[p][:, R0, :].unsqueeze(2).to_broadcast([P, F, F]),
                                       ALU.mult).then_inc(outer_ready, 1)
                elif back:
                    pool.memset(idle[:, :], 0.0)
                if back:
                    times_e(ways1[q][:, :, :], n + 1, slice(FRONT_WAYS, WAYS)).then_inc(ways1_ready, 1)
                if prev:
                    pool.wait_ge(inv1_ready, n)
                    normalise(n - 1, q, 0)
                    normalise(n - 1, q, 2)
                    normalise(n - 1, q, 3)
                if front:
                    pool.wait_ge(norm0_ready, n + 3)
                    pool.tensor_tensor(x0, x0, ways0[p][:, V0:V0 + 1, :].to_broadcast([P, F, F]),
                                       ALU.mult).then_inc(weighed0, 1)
                if prev:
                    normalise(n - 1, q, 4)

            def once(half, turn_no):
                now[0] = half
                t = half // 2 + 1
                if half < HALVES and t < BLOCKS:
                    lot = 2 * (half % 2) + turn_no
                    if lot < 3:
                        gather(t, lot * F // 3, (lot + 1) * F // 3)
                    else:
                        pool.wait_ge(emb_ready, ROUNDS * (t + 1))

            tiles(pool, step, once)

        @block.vector
        def _(dve):
            dve.memset(cw0[PAIRS0 % P:P, TCHUNKS - 1, :], 0.0).then_inc(pads_cleared, 1)
            dve.wait_ge(ident_ready, 1)
            dve.tensor_reduce(group_sel[:, :], ident[:, :].rearrange("p (b k) -> p b k", k=K), X, ALU.add).then_inc(sel_ready, 1)
            dve.tensor_tensor(fold[:, :], ident[:, 0:HALF_ROWS], ident[:, HALF_ROWS:P], ALU.add).then_inc(sel_ready, 1)
            dve.wait_ge(loads_in, LOADS)

            def exponents(n, p, c):
                need(dve, pooled_done, NP * (n - 2) + FREED[c])
                mid, hi = (c + 1) * CHUNK_F - SCALED[c], (c + 1) * CHUNK_F
                for f in range(c * CHUNK_F, mid):
                    dve.scalar_tensor_tensor(out=x1[p][:, f, :], in0=r1[:, :], scalar=ways1[p][:, A, f:f + 1],
                                             in1=top1, op0=ALU.mult, op1=ALU.subtract)
                dve.wait_ge(scaled_ready, CHUNKS * n + c + 1)
                dve.tensor_tensor(x1[p][:, mid:hi, :], x1[p][:, mid:hi, :],
                                  top1.unsqueeze(1).to_broadcast([P, hi - mid, G1]), ALU.subtract).then_inc(args_ready, 1)

            def step(n, p):
                here, prev, done, back, front = stages(n)
                q = 1 - p
                if here:
                    dve.wait_ge(ways1_ready, n + 1)
                    exponents(n, p, 0)
                if prev:
                    dve.wait_ge(exp1_ready, CHUNKS * n)
                    dve.tensor_reduce(part1[:, :], x1[q][:, SUM_PE:F, :].rearrange("p f g -> p g f"), X,
                                      ALU.add).then_inc(part1_ready, 1)
                if here:
                    exponents(n, p, 1)
                if prev:
                    dve.wait_ge(sum1_done, n)
                    dve.wait_ge(part1_ready, n)
                    dve.tensor_tensor(part1[:, :], sum1[q], part1[:, :], ALU.add).then_inc(total1_ready, 1)
                    dve.wait_ge(total1_ready, n)
                    need(dve, norm1_p, (NP - 1) * (n - 1))
                    need(dve, norm1_v, n - 1)
                    dve.reciprocal(inv1[:, :], part1[:, :]).then_inc(inv1_ready, 1)
                    dve.wait_ge(inv1_ready, n)
                    piece = x1[q][:, PIECES[V_PIECE]:PIECES[V_PIECE + 1], :]
                    dve.tensor_tensor(piece, piece, inv1[:, :].unsqueeze(1)
                                      .to_broadcast([P, PIECES[V_PIECE + 1] - PIECES[V_PIECE], G1]),
                                      ALU.mult).then_inc(norm1_v, 1)
                if front:
                    dve.wait_ge(ways0_ready, n + 3)
                    dve.tensor_reduce(ends[p][:, 0, :], ways0[p][:, A0:A1 + 1, :], X, ALU.max).then_inc(ends_ready, 1)
                    dve.tensor_reduce(ends[p][:, 1, :], ways0[p][:, A0:A1 + 1, :], X, ALU.min).then_inc(ends_ready, 1)
                    dve.wait_ge(ends_ready, 2 * (n + 3))
                    dve.tensor_scalar(low0[:, :], ways0[p][:, R0, :], ends[p][:, 1, 0:1], None, ALU.mult).then_inc(low0_ready, 1)
                    dve.wait_ge(low0_ready, n + 3)
                    dve.scalar_tensor_tensor(out=top0, in0=ways0[p][:, R0, :], scalar=ends[p][:, 0, 0:1], in1=low0[:, :],
                                             op0=ALU.mult, op1=ALU.max).then_inc(top0_ready, 1)
                    dve.wait_ge(top0_ready, n + 3)
                    dve.wait_ge(outer_ready, n + 3)
                    dve.tensor_tensor(x0, x0, top0.unsqueeze(2).to_broadcast([P, F, F]),
                                      ALU.subtract).then_inc(shifted0, 1)
                if here:
                    exponents(n, p, 2)
                if front:
                    dve.wait_ge(exp0_ready, n + 3)
                    dve.tensor_reduce(sum0[:, :], x0, X, ALU.add).then_inc(sum0_ready, 1)
                    dve.wait_ge(sum0_ready, n + 3)
                    dve.reciprocal(rcp0, sum0[:, :]).then_inc(rcp0_ready, 1)
                    dve.wait_ge(rcp0_ready, n + 3)
                    dve.tensor_tensor(x0, x0, rcp0.unsqueeze(2).to_broadcast([P, F, F]),
                                      ALU.mult).then_inc(norm0_ready, 1)
                if here:
                    exponents(n, p, 3)
                if back:
                    dve.wait_ge(res_copied, n + 2)
                    need(dve, args_ready, CHUNKS * (n + 1))
                    dve.tensor_tensor(r1[:, :], res[:, :], wq1[:, :], ALU.mult).then_inc(r1_ready, 1)
                    dve.wait_ge(r1_ready, n + 2)
                    dve.tensor_scalar(low1[:, :], r1[:, :], ends[q][:, 1, 1:2], None, ALU.mult).then_inc(low1_ready, 1)
                    dve.wait_ge(low1_ready, n + 2)
                    dve.scalar_tensor_tensor(out=top1, in0=r1[:, :], scalar=ends[q][:, 0, 1:2], in1=low1[:, :],
                                             op0=ALU.mult, op1=ALU.max).then_inc(top1_ready, 1)
                    dve.wait_ge(top1_ready, n + 2)
            tiles(dve, step, lambda half, turn_no: None)

        @block.scalar
        def _(act):
            act.wait_ge(loads_in, LOADS)

            def keep_rows(t):
                for lo in range(0, F, ROUND_F):
                    hi = min(lo + ROUND_F, F)
                    act.wait_ge(emb_turned, F * t + hi)
                    src = misc[:, 0:(hi - lo) * BLOCK_TILES].rearrange("p (f t) -> p t f", t=BLOCK_TILES)
                    base = t % 2 * BLOCK_TILES
                    if t == 2:
                        act.copy(emb[:, RING:RING + AHEAD, lo:hi], src[:, 0:AHEAD, :])
                    act.copy(emb[:, base:base + BLOCK_TILES, lo:hi], src).then_inc(emb_ready, 1)

            keep_rows(0)
            now = [0]

            def scale(n, p, c):
                if c == 0:
                    act.wait_ge(r1_ready, n + 1)
                    act.wait_ge(ways1_ready, n + 1)
                need(act, pooled_done, NP * (n - 2) + FREED[c])
                for f in range((c + 1) * CHUNK_F - SCALED[c], (c + 1) * CHUNK_F):
                    last = act.activation(x1[p][:, f, :], r1[:, :], ACT.Copy, scale=ways1[p][:, A, f:f + 1])
                last.then_inc(scaled_ready, 1)

            def exp1(n, p, c):
                act.wait_ge(args_ready, CHUNKS * n + c + 1)
                part = x1[p][:, c * CHUNK_F:(c + 1) * CHUNK_F, :]
                act.activation(part, part, ACT.Exp).then_inc(exp1_ready, 1)

            def keep_turned0(n, g):
                if g == 0:
                    need(act, res_done, n)
                act.wait_ge(turned0, TGROUPS * n + g + 1)
                lo, hi = TGROUP * g, min(TGROUP * (g + 1), TCHUNKS)
                act.copy(x0t[:, lo:hi, :], turn[g % 2][:, 0:(hi - lo) * P].rearrange("p (c q) -> p c q", q=P)
                         ).then_inc(x0t_ready, 1)

            def step(n, p):
                here, prev, done, back, front = stages(n)
                if here:
                    scale(n, p, 1)
                if back:
                    keep_turned0(n + 1, 0)
                    keep_turned0(n + 1, 1)
                if here:
                    exp1(n, p, 0)
                if back:
                    keep_turned0(n + 1, 2)
                    keep_turned0(n + 1, 3)
                if done:
                    act.wait_ge(pooled_done, NP * (n - 1))
                    need(act, pooled_turned, n - 2)
                    act.copy(pooled[:, :, :], pooled_view[:, :, 0:G1]).then_inc(pooled_copied, 1)
                if here:
                    scale(n, p, 2)
                if here:
                    exp1(n, p, 1)
                if front:
                    act.wait_ge(shifted0, n + 3)
                    act.activation(x0, x0, ACT.Exp).then_inc(exp0_ready, 1)
                if done:
                    act.wait_ge(pooled_turned, n - 1)
                    if isinstance(n, int):
                        t = (n - 2) % HALF_TILES
                        spot = lambda v: v[:, :, :, t]
                        need(act, z1_done, (n - 2) // HALF_TILES)
                    else:
                        spot = lambda v: v[:, :, :, bass.ds(n - 2 - now[0] * HALF_TILES, 1)].rearrange("p c q o -> p c (q o)")
                        need(act, z1_done, now[0])
                    flat = pooled_t[:, :, :, :, :].rearrange("p c f b t -> p c (f b) t")
                    act.copy(spot(flat[:, :, 0:REGION0_F * GROUPS, :]), pt_ps[:, :, 0, :]).then_inc(pooled_kept, 1)
                    v = spot(flat[:, :, REGION0_F * GROUPS:F * GROUPS, :]).rearrange("p c (j x) -> p c j x", j=4)
                    act.copy(v, pt_ps[:, :, 1, :].rearrange("p c (j x) -> p c j x", j=4)[:, :, :, 0:8]).then_inc(pooled_kept, 1)
                if here:
                    scale(n, p, 3)
                if back:
                    act.wait_ge(res_done, n + 2)
                    need(act, z0_summed, n + 1)
                    need(act, r1_ready, n + 1)
                    act.copy(res[:, :], res_ps).then_inc(res_copied, 1)
                if here:
                    exp1(n, p, 2)
                if here:
                    exp1(n, p, 3)
                if back:
                    act.wait_ge(z0_summed, n + 2)
                    act.copy(zt[:, 0:2, bass.ds(GROUPS * (n + 1), GROUPS)], z0_ps).then_inc(z0_kept, 1)
                if back:
                    scale(n + 1, 1 - p, 0)

            def once(half, turn_no):
                now[0] = half
                if half and turn_no:
                    act.wait_ge(z1_done, half)
                    need(act, z1_turned, half - 1)
                    act.copy(z1[:, :], misc[:, 0:G1]).then_inc(z1_copied, 1)
                    act.wait_ge(z1_turned, half)
                    dst = zt[:, 2:4, (half - 1) * HALF_ROWS:half * HALF_ROWS].rearrange("p c (t b) -> p c b t", b=GROUPS)
                    for c in range(2):
                        act.copy(dst[:, c], misc[0:HG, 256 + HALF_ROWS * c:256 + HALF_ROWS * (c + 1)]
                                 .rearrange("p (b t) -> p b t", t=HALF_TILES)).then_inc(z1_kept, 1)
                if half < HALVES and half % 2 and turn_no and half // 2 + 1 < BLOCKS:
                    keep_rows(half // 2 + 1)

            tiles(act, step, once)

            for m in range(H1 // P):
                act.wait_ge(h1_done, m + 1)
                act.activation(h1t[:, m, :], turn[m % 2][:, :], ACT.Relu, bias=b1[:, m:m + 1]).then_inc(h1_ready, 1)
            for m in range(H2 // P):
                act.wait_ge(h2_done, m + 1)
                act.activation(h2t[:, m, :], turn[m % 2][:, :], ACT.Relu, bias=b2[:, m:m + 1]).then_inc(h2_ready, 1)
            act.wait_ge(y_done, 1)
            act.copy(y_sb.rearrange("o (x g t) -> o x t g", g=GROUPS, t=BLOCK_TILES),
                     res_bank[0:1, :].rearrange("o (x t g) -> o x t g", g=GROUPS, t=BLOCK_TILES)).then_inc(y_ready, 1)

        @block.tensor
        def _(pe):
            pe.wait_ge(ident_ready, 1)
            pe.wait_ge(pads_cleared, 2)
            pe.wait_ge(sel_ready, 2)
            pe.wait_ge(loads_in, LOADS)

            def turn_rows(t):
                for f in range(F):
                    r = f // ROUND_F
                    if f % ROUND_F == 0:
                        pe.wait_ge(rows_in[r], 16 * (min(F, f + ROUND_F) - f) * (t + 1))
                        need(pe, emb_ready, ROUNDS * t + r)
                        if t and f == 0:
                            pe.wait_ge(z1_kept, 2 * (2 * t - 1))
                    at_f = slice(f % ROUND_F * BLOCK_TILES, (f % ROUND_F + 1) * BLOCK_TILES)
                    for g in range(GROUPS):
                        at_g = slice(g * K, (g + 1) * K)
                        last = pe.matmul(misc[at_g, at_f], rows[:, f, :],
                                         ident[:, at_g], start=True, stop=True)
                    last.then_inc(emb_turned, 1)

            turn_rows(0)

            def sums(n, p, c):
                pe.wait_ge(exp1_ready, CHUNKS * n + c + 1)
                if c == 0:
                    need(pe, total1_ready, n - 1)
                hi = min(SUM_PE, (c + 1) * CHUNK_F)
                for f in range(c * CHUNK_F, hi):
                    last = pe.matmul(sum1[p], ident[:, :], x1[p][:, f, :], start=f == 0, stop=f == SUM_PE - 1)
                if hi == SUM_PE:
                    last.then_inc(sum1_done, 1)

            def turn0(n, g):
                if g == 0:
                    pe.wait_ge(weighed0, n + 1)
                need(pe, x0t_ready, TGROUPS * n + g - 1)
                for c in range(TGROUP * g, min(TGROUP * (g + 1), TCHUNKS)):
                    last = pe.transpose(turn[g % 2][:, (c % TGROUP) * P:(c % TGROUP + 1) * P],
                                        x0_pad[:, c * P:(c + 1) * P], ident[:, :])
                last.then_inc(turned0, 1)

            def pool_k(n, q, i):
                if i == 0:
                    pe.wait_ge(vsel_ready, 2 * (n + 1))
                    need(pe, pooled_kept, 2 * n)
                if i == V_PIECE:
                    pe.wait_ge(norm1_v, n + 1)
                else:
                    pe.wait_ge(norm1_p, (NP - 1) * n + i + (i < V_PIECE))
                for f in range(PIECES[i], PIECES[i + 1]):
                    j, region = f % 4, f // REGION0_F
                    row, count = (f - REGION0_F * region) // 4, (REGION0_F, F - REGION0_F)[region] // 4
                    last = pe.matmul(pooled_ps[32 * j:32 * (j + 1), 256 * region:256 * region + G1],
                                     vsel[:, 32 * f:32 * (f + 1)], x1[q][:, f, :],
                                     start=row == 0, stop=row == count - 1)
                last.then_inc(pooled_done, 1)

            Z1_SLOTS = -(-2 * F // 3)
            SLOTS_IN = [(c, slot) for c in range(2) for slot in range(F)]

            def z1_part(half, part):
                lo, hi = part * Z1_SLOTS, min(2 * F, (part + 1) * Z1_SLOTS)
                if lo == 0:
                    pe.wait_ge(cw1_in, 32)
                    pe.wait_ge(pooled_kept, 2 * HALF_TILES * half)
                    need(pe, z1_kept, 2 * (half - 1))
                    pe.wait_ge(emb_ready, ROUNDS * min(BLOCKS, 1 + half // 2))
                flat = pooled_t[:, :, :, :, :].rearrange("p c f b t -> p c f (b t)")
                for c, slot in SLOTS_IN[lo:hi]:
                    if slot < REGION0_F:
                        f = slot // 8 + 4 * (slot % 8)
                    else:
                        f = REGION0_F + (slot - REGION0_F) // 2 + 4 * (slot % 2)
                    side = slot % 2
                    last = pe.matmul(misc[HALF_ROWS * side:HALF_ROWS * (side + 1), 0:G1], flat[:, c, slot, :],
                                     cw1[:, c, f, :], start=c == 0 and slot < 2, stop=c == 1 and slot >= F - 2)
                if hi == 2 * F:
                    last.then_inc(z1_done, 1)

            def step(n, p):
                here, prev, done, back, front = stages(n)
                turning = isinstance(n, int) and n > 1 and n % HALF_TILES == 1
                q = 1 - p
                if prev:
                    sums(n - 1, q, 3)
                if back:
                    turn0(n + 1, 0)
                    turn0(n + 1, 1)
                if done:
                    pool_k(n - 2, p, 4)
                if back:
                    turn0(n + 1, 2)
                    turn0(n + 1, 3)
                if back:
                    need(pe, z0_kept, n + 1)
                    for c in range(TCHUNKS):
                        if c % TGROUP == 0:
                            pe.wait_ge(x0t_ready, TGROUPS * (n + 1) + c // TGROUP + 1)
                        last = pe.matmul(res_ps, x0t[:, c, :], cw0[:, c, :], start=c == 0, stop=c == TCHUNKS - 1)
                    last.then_inc(res_done, 1)
                if here:
                    sums(n, p, 0)
                if done:
                    pe.wait_ge(pooled_copied, n - 1)
                    for c in range(2):
                        for r in range(2):
                            last = pe.transpose(pt_ps[:, c, r, :], pooled[:, r, c * HG:(c + 1) * HG], ident[:, :])
                    last.then_inc(pooled_turned, 1)
                if turning:
                    z1_part(n // HALF_TILES, 0)
                if prev:
                    pool_k(n - 1, q, 0)
                    pool_k(n - 1, q, 1)
                if here:
                    sums(n, p, 1)
                if prev:
                    pool_k(n - 1, q, 2)
                if turning:
                    z1_part(n // HALF_TILES, 1)
                if back:
                    pe.wait_ge(res_copied, n + 2)
                    for c in range(2):
                        last = pe.matmul(z0_ps[:, c, :], res[:, c * HG:(c + 1) * HG], group_sel[:, :], start=True, stop=True)
                    last.then_inc(z0_summed, 1)
                if here:
                    sums(n, p, 2)
                if prev:
                    pool_k(n - 1, q, 3)
                if turning:
                    z1_part(n // HALF_TILES, 2)

            def z1_fold(half):
                pe.wait_ge(z1_copied, half)
                for c in range(2):
                    last = pe.matmul(misc[0:HG, 256 + HALF_ROWS * c:256 + HALF_ROWS * (c + 1)],
                                     z1[:, c * HG:(c + 1) * HG], fold[:, :], start=True, stop=True)
                last.then_inc(z1_turned, 1)

            def once(half, turn_no):
                if half and turn_no:
                    z1_fold(half)
                if half < HALVES and half % 2 and turn_no and half // 2 + 1 < BLOCKS:
                    turn_rows(half // 2 + 1)

            tiles(pe, step, once)

            pe.wait_ge(mlp_in, 64)
            pe.wait_ge(z1_kept, 2 * HALVES)
            pe.wait_ge(z0_kept, TILES)
            for m in range(H1 // P):
                need(pe, h1_ready, m - 1)
                cols = slice(m * P, (m + 1) * P)
                for c in range(4):
                    pe.matmul(turn[m % 2][:, :], w1[:, c, cols], zt[:, c, :], start=c == 0, stop=False)
                pe.matmul(turn[m % 2][:, :], w1d[:, cols], dense_t, start=False, stop=True).then_inc(h1_done, 1)
            pe.wait_ge(h1_ready, H1 // P)
            for m in range(H2 // P):
                for c in range(H1 // P):
                    last = pe.matmul(turn[m % 2][:, :], w2[:, c, m * P:(m + 1) * P], h1t[:, c, :],
                                     start=c == 0, stop=c == H1 // P - 1)
                last.then_inc(h2_done, 1)
            pe.wait_ge(h2_ready, H2 // P)
            for c in range(H2 // P):
                last = pe.matmul(res_bank[0:1, :], w3[:, c:c + 1], h2t[:, c, :], start=c == 0, stop=c == H2 // P - 1)
            last.then_inc(y_done, 1)


def kernel(**inputs):
    import numpy as np
    import concourse.bacc as bacc
    from concourse import mybir
    from concourse.bass_utils import run_bass_kernel_spmd

    a = {k: np.asarray(v) for k, v in inputs.items()}
    by_k = lambda name: a[name][0].T
    laid = {
        "ids": a["ids"],
        "field_w": np.stack([by_k(f"L0_rec_{w}") for w in ("wk0", "wk1", "wq0", "wv0", "wk1", "wv1")], axis=1),
        "wq1": by_k("L0_rec_wq1"),
        "cw0": a["L0_rec_cw0"][0].reshape(F, F, G1).transpose(1, 0, 2).reshape(PAIRS0, G1),
        "cw1": a["L0_rec_cw1"][0].reshape(F, 2, HG, G1).transpose(2, 1, 0, 3),
        "dense_t": a["dense_ctx"].reshape(BLOCKS, GROUPS, BLOCK_TILES, DENSE).transpose(3, 0, 2, 1).reshape(DENSE, B),
        "w1": a["W_top1"],
        "b1": a["b_top1"].reshape(H1 // P, P).T,
        "w2": a["W_top2"],
        "b2": a["b_top2"].reshape(H2 // P, P).T,
        "w3": a["W_top3"].reshape(H2 // P, P).T,
    }
    for f in range(F):
        laid[f"tbl_{f}"] = a[f"tbl_{f}"]
    laid = {k: np.ascontiguousarray(v) for k, v in laid.items()}

    nc = bacc.Bacc("TRN2", target_bir_lowering=False, num_devices=1)
    dram = {k: nc.dram_tensor(f"in_{k}", v.shape, mybir.dt.from_np(v.dtype), kind="ExternalInput").ap() for k, v in laid.items()}
    out = nc.dram_tensor("out", (B, 1), mybir.dt.float32, kind="ExternalOutput").ap()
    build(nc, dram, out.rearrange("b o -> o b"))
    r = run_bass_kernel_spmd(nc, [{f"in_{k}": v for k, v in laid.items()}], core_ids=[0])
    return r.results[0]["out"]
```

```python
B, F, K, G1 = 512, 40, 32, 200
DENSE, H1, H2 = 16, 512, 256
P = 128
GROUPS = P // K
BLOCKS = B // P
TILES = B // GROUPS
BLOCK_TILES = P // GROUPS
HALF_TILES = 16
HALVES = TILES // HALF_TILES
HALF_ROWS = HALF_TILES * GROUPS
PAIRS0 = F * F
CHUNKS = 4
CHUNK_F = F // CHUNKS
SCALED = (3, 8, 8, 8)
PIECES = (0, 8, 17, 25, 33, 40)
NP = len(PIECES) - 1
FREED = tuple(next(i for i in range(NP) if PIECES[i + 1] >= (c + 1) * CHUNK_F) + 1 for c in range(CHUNKS))
TCHUNKS = -(-PAIRS0 // P)
TGROUP = 4
TGROUPS = -(-TCHUNKS // TGROUP)
HG = G1 // 2
WAYS = 6
FRONT_WAYS = 4
A0, A1, R0, V0 = range(FRONT_WAYS)
A, V = range(WAYS - FRONT_WAYS)
AHEAD = 2
RING = 2 * BLOCK_TILES
REGION0_F = 32
ROUND_F = 16
ROUNDS = -(-F // ROUND_F)
LOTS = (17, 23)
EARLY_SUM = slice(CHUNK_F, 3 * CHUNK_F)
WITH_GATHER = [BLOCK_TILES * i - 1 for i in range(1, BLOCKS - 1)]


def opens_half(n):
    return isinstance(n, int) and 0 < n < TILES and n % HALF_TILES == 0


def sums_half(n):
    return isinstance(n, int) and n > 1 and n % HALF_TILES == 1


def turns_rows(n):
    return opens_half(n) and n // HALF_TILES % 2 == 1 and n // (2 * HALF_TILES) + 1 < BLOCKS


def by_vector(n):
    if not isinstance(n, int):
        return (1,)
    if n == TILES - 1 or opens_half(n):
        return (0, 1, 2)
    return (0, 1) if n in WITH_GATHER else (1,)


def sum_pe(n):
    return 30 if opens_half(n) else 35


def build(nc, dram, out):
    from contextlib import ExitStack

    import concourse.bass as bass
    from concourse import mybir

    fp32 = mybir.dt.float32
    ALU = mybir.AluOpType
    ACT = mybir.ActivationFunctionType
    X = mybir.AxisListType.X

    with ExitStack() as ctx:
        def sb(name, shape, dt=fp32):
            return ctx.enter_context(nc.sbuf_tensor(name, shape, dt))

        def bank(name):
            return ctx.enter_context(nc.psum_tensor(name, [P, 512], fp32))

        def sem(name):
            return ctx.enter_context(nc.semaphore(name))

        ident = sb("ident", [P, P])
        group_sel = sb("group_sel", [P, GROUPS])
        fold = sb("fold", [P, HALF_ROWS])
        ids_sb = sb("ids_sb", [P, BLOCKS, F], mybir.dt.int32)
        field_w = sb("field_w", [P, WAYS, F])
        wq1 = sb("wq1", [P, G1])
        cw0 = sb("cw0", [P, TCHUNKS, G1])
        cw1 = sb("cw1", [HG, 2, F, G1])
        rows = sb("rows", [P, F, K])
        emb = sb("emb", [P, RING + AHEAD, F])
        ways0 = [sb(f"ways0_{i}", [P, FRONT_WAYS, F]) for i in range(2)]
        ways1 = [sb(f"ways1_{i}", [P, WAYS - FRONT_WAYS, F]) for i in range(2)]
        ends = [sb(f"ends{i}", [P, 2, 2]) for i in range(2)]
        x0_pad = sb("x0_pad", [P, TCHUNKS * P])
        x0 = x0_pad[:, 0:PAIRS0].rearrange("p (g f) -> p g f", f=F)
        x0t = sb("x0t", [P, TCHUNKS, P])
        low0 = sb("low0", [P, F])
        sum0 = sb("sum0", [P, F])
        res = sb("res", [P, G1])
        r1 = sb("r1", [P, G1])
        low1 = sb("low1", [P, G1])
        part1 = low1
        x1 = [sb(f"x1_{i}", [P, F, G1]) for i in range(2)]
        inv1 = sb("inv1", [P, G1])
        vsel = sb("vsel", [P, 1288])
        pooled = sb("pooled", [P, 2, G1])
        pooled_t = sb("pooled_t", [HG, 2, F, GROUPS, HALF_TILES])
        z1 = sb("z1", [P, G1])
        early = z1
        zt = sb("zt", [HG, 4, B])
        b1 = sb("b1", [P, H1 // P])
        b2 = sb("b2", [P, H2 // P])
        w3 = sb("w3", [P, H2 // P])

        spare = x1[0][:, :, :].rearrange("p f g -> p (f g)")
        w1 = spare[0:HG, 0:4 * H1].rearrange("p (c n) -> p c n", c=4)
        w1d = spare[0:DENSE, 4 * H1:5 * H1]
        w2 = spare[:, 5 * H1:5 * H1 + 4 * H2].rearrange("p (c n) -> p c n", c=4)
        at = 5 * H1 + 4 * H2
        h1t = spare[:, at:at + 4 * B].rearrange("p (c n) -> p c n", c=4)
        dense_t = spare[0:DENSE, at + 6 * B:at + 7 * B]
        y_sb = spare[0:1, at + 7 * B:at + 8 * B]
        h2t = spare[:, at + 4 * B:at + 6 * B].rearrange("p (c n) -> p c n", c=2)

        turn = [bank("turn0"), bank("turn1")]
        res_bank = bank("res_bank")
        res_ps = res_bank[:, 0:G1]
        z0_ps = res_bank[0:HG, 256:256 + 2 * GROUPS].rearrange("p (c b) -> p c b", c=2)
        sum1 = [bank(f"sum1_{i}")[:, 0:G1] for i in range(2)]
        small = bank("small")
        top1 = small[:, 0:G1]
        top0 = small[:, 416:416 + F]
        rcp0 = small[:, 464:464 + F]
        pooled_ps = bank("pooled_ps")
        pooled_view = pooled_ps[:, :].rearrange("p (r g) -> p r g", r=2)
        pt_ps = pooled_ps[0:HG, :].rearrange("p (c r q) -> p c r q", c=2, r=2)
        misc = bank("misc")

        ids_in = sem("ids_in")
        loads_in = sem("loads_in")
        cw1_in = sem("cw1_in")
        mlp_in = sem("mlp_in")
        pads_cleared = sem("pads_cleared")
        ident_cleared = sem("ident_cleared")
        ident_ready = sem("ident_ready")
        sel_ready = sem("sel_ready")
        vsel_cleared = sem("vsel_cleared")
        rows_in = [sem(f"rows_in{i}") for i in range(ROUNDS)]
        emb_turned = sem("emb_turned")
        emb_ready = sem("emb_ready")
        ways0_ready = sem("ways0_ready")
        ways1_ready = sem("ways1_ready")
        scaled_ready = sem("scaled_ready")
        part1_ready = sem("part1_ready")
        total1_ready = sem("total1_ready")
        early_ready = sem("early_ready")
        outer_ready = sem("outer_ready")
        ends_ready = sem("ends_ready")
        low0_ready = sem("low0_ready")
        top0_ready = sem("top0_ready")
        shifted0 = sem("shifted0")
        exp0_ready = sem("exp0_ready")
        sum0_ready = sem("sum0_ready")
        rcp0_ready = sem("rcp0_ready")
        norm0_ready = sem("norm0_ready")
        weighed0 = sem("weighed0")
        turned0 = sem("turned0")
        x0t_ready = sem("x0t_ready")
        res_done = sem("res_done")
        res_copied = sem("res_copied")
        z0_summed = sem("z0_summed")
        z0_kept = sem("z0_kept")
        r1_ready = sem("r1_ready")
        low1_ready = sem("low1_ready")
        top1_ready = sem("top1_ready")
        terms_ready = sem("terms_ready")
        args_ready = sem("args_ready")
        exp1_ready = sem("exp1_ready")
        sum1_done = sem("sum1_done")
        inv1_ready = sem("inv1_ready")
        norm1_ready = [sem(f"norm1_ready{i}") for i in range(NP)]
        vsel_ready = sem("vsel_ready")
        pooled_done = sem("pooled_done")
        pooled_copied = sem("pooled_copied")
        pooled_turned = sem("pooled_turned")
        pooled_kept = sem("pooled_kept")
        z1_done = sem("z1_done")
        z1_copied = sem("z1_copied")
        z1_turned = sem("z1_turned")
        z1_kept = sem("z1_kept")
        h1_done = sem("h1_done")
        h1_ready = sem("h1_ready")
        h2_done = sem("h2_done")
        h2_ready = sem("h2_ready")
        y_done = sem("y_done")
        y_ready = sem("y_ready")
        stored = sem("stored")

        def need(eng, semaphore, count):
            if not isinstance(count, int) or count > 0:
                eng.wait_ge(semaphore, count)

        def tiles(eng, step, once):
            for n in range(-AHEAD, 0):
                step(n, n % 2)
            for half in range(HALVES):
                first = half * HALF_TILES
                step(first, 0)
                once(half, 0)
                step(first + 1, 1)
                once(half, 1)
                pairs = HALF_TILES // 2
                peeled = half == HALVES - 1
                with eng.Fori(1, pairs - peeled) as i:
                    step(first + 2 * i, 0)
                    step(first + 2 * i + 1, 1)
            step(TILES - 2, 0)
            step(TILES - 1, 1)
            step(TILES, 0)
            once(HALVES, 0)
            step(TILES + 1, 1)
            once(HALVES, 1)

        def stages(n):
            known = isinstance(n, int)
            return [not known or 0 <= n + ahead < TILES for ahead in (0, -1, -2, 1, 2)]

        def slot_of(m, half):
            return m % RING if isinstance(m, int) else m - half // 4 * RING

        block = ctx.enter_context(nc.Block())

        @block.sync
        def _(sp):
            sp.dma_start(ids_sb[:, :, :], dram["ids"].rearrange("(t p) f -> p t f", p=P)).then_inc(ids_in, 16)
            for g in range(GROUPS):
                at_g = slice(g * K, (g + 1) * K)
                sp.dma_start(field_w[at_g, :, :], dram["field_w"]).then_inc(loads_in, 16)
                sp.dma_start(wq1[at_g, :], dram["wq1"]).then_inc(loads_in, 16)
            full = PAIRS0 // P
            sp.dma_start(cw0[:, 0:full, :], dram["cw0"][0:full * P, :].rearrange("(c p) j -> p c j", p=P)).then_inc(loads_in, 16)
            sp.dma_start(cw0[0:PAIRS0 - full * P, full, :], dram["cw0"][full * P:PAIRS0, :]).then_inc(loads_in, 16)
            sp.dma_start(b1[:, :], dram["b1"]).then_inc(loads_in, 16)
            sp.dma_start(b2[:, :], dram["b2"]).then_inc(loads_in, 16)
            sp.dma_start(w3[:, :], dram["w3"]).then_inc(loads_in, 16)
            for c in range(2):
                sp.dma_start(cw1[:, c, :, :], dram["cw1"][:, c, :, :]).then_inc(cw1_in, 16)
            sp.wait_ge(pooled_done, NP * (TILES - 1))
            sp.dma_start(w1, dram["w1"][0:4 * HG, :].rearrange("(c p) n -> p c n", p=HG)).then_inc(mlp_in, 16)
            sp.dma_start(dense_t, dram["dense_t"]).then_inc(mlp_in, 16)
            sp.dma_start(w1d, dram["w1"][4 * HG:4 * HG + DENSE, :]).then_inc(mlp_in, 16)
            sp.dma_start(w2, dram["w2"].rearrange("(c p) n -> p c n", p=P)).then_inc(mlp_in, 16)
            sp.wait_ge(y_ready, 1)
            sp.dma_start(out, y_sb).then_inc(stored, 16)
            sp.wait_ge(stored, 16)
        LOADS = 16 * (2 * GROUPS + 2 + 3)

        @block.gpsimd
        def _(pool):
            pool.memset(ident[:, :], 0.0).then_inc(ident_cleared, 1)
            pool.wait_ge(ident_cleared, 1)
            pool.affine_select(out=ident[:, :], in_=ident[:, :], compare_op=ALU.not_equal, fill=1.0,
                               base=0, pattern=[[-1, P]], channel_multiplier=1).then_inc(ident_ready, 1)
            pool.memset(x0_pad[:, PAIRS0:], 0.0).then_inc(pads_cleared, 1)
            pool.memset(vsel[:, :], 0.0).then_inc(vsel_cleared, 1)
            pool.wait_ge(ids_in, 16)

            def gather(t, lo, hi):
                for f in range(lo, hi):
                    pool.indirect_dma_start(
                        out=rows[:, f, :], out_offset=None, in_=dram[f"tbl_{f}"],
                        in_offset=bass.IndirectOffsetOnAxis(ap=ids_sb[:, t, f:f + 1], axis=0),
                    ).then_inc(rows_in[f // ROUND_F], 16)

            gather(0, 0, F)
            pool.wait_ge(loads_in, LOADS)
            pool.wait_ge(sel_ready, 2)
            pool.wait_ge(vsel_cleared, 1)
            now = [0]

            def normalise(n, q, i):
                if i in by_vector(n):
                    return
                part = x1[q][:, PIECES[i]:PIECES[i + 1], :]
                pool.tensor_tensor(part, part, inv1[:, :].unsqueeze(1).to_broadcast([P, PIECES[i + 1] - PIECES[i], G1]),
                                   ALU.mult).then_inc(norm1_ready[i], 1)

            def gather_share(n, share):
                if not isinstance(n, int) or n >= TILES:
                    return
                half, second = n // HALF_TILES, n % HALF_TILES == 1
                if n <= 1:
                    t = 1
                    lo, hi = (33, F) if n == 1 else (11 * (n + AHEAD), 11 * (n + AHEAD + 1))
                elif half % 2 and second:
                    t = half // 2 + 2
                    lo, hi = 0, LOTS[0]
                elif half % 2 == 0 and n % HALF_TILES <= 1:
                    t = half // 2 + 1
                    lo, hi = (LOTS[1], F) if second else LOTS
                else:
                    return
                if t < BLOCKS:
                    if share == 0:
                        pool.wait_ge(emb_turned, F * t)
                    cuts = [lo + (hi - lo) * of_ten // 10 for of_ten in (0, 4, 7, 8, 10)]
                    gather(t, cuts[share], cuts[share + 1])

            def times_e(dst, m, ways):
                at = slot_of(m, now[0])
                count = ways.stop - ways.start
                return pool.tensor_tensor(dst, emb[:, bass.ds(at, 1), :].to_broadcast([P, count, F]),
                                          field_w[:, ways, :], ALU.mult)

            def step(n, p):
                here, prev, done, back, front = stages(n)
                q = 1 - p
                if isinstance(n, int) and (front or back):
                    newest = min(n + AHEAD, TILES - 1) // BLOCK_TILES
                    pool.wait_ge(emb_ready, ROUNDS * (newest + 1))
                if front:
                    times_e(ways0[p][:, :, :], n + 2, slice(0, FRONT_WAYS)).then_inc(ways0_ready, 1)
                    pool.wait_ge(ways0_ready, n + 3)
                    need(pool, turned0, TGROUPS * (n + 2))
                    pool.tensor_tensor(x0, ways0[p][:, A0:A0 + 1, :].to_broadcast([P, F, F]),
                                       ways0[p][:, R0, :].unsqueeze(2).to_broadcast([P, F, F]),
                                       ALU.mult).then_inc(outer_ready, 1)
                if prev:
                    need(pool, pooled_done, NP * (n - 1))
                    for lo, count, base in ((0, 8, 0), (8, 2, 8 * P)):
                        pool.tensor_tensor(
                            vsel[:, base:base + 132 * count].rearrange("p (i x) -> p i x", x=132)[:, :, 0:P]
                            .rearrange("p i (j c) -> p i j c", c=32)[:, :, :, 0:GROUPS],
                            ways1[q][:, V, 4 * lo:4 * (lo + count)].rearrange("p (i j) -> p i j", j=4)
                            .unsqueeze(3).to_broadcast([P, count, 4, GROUPS]),
                            group_sel[:, :].unsqueeze(1).unsqueeze(1).to_broadcast([P, count, 4, GROUPS]),
                            ALU.mult).then_inc(vsel_ready, 1)
                    pool.wait_ge(inv1_ready, n)
                    pool.wait_ge(args_ready, CHUNKS * n)
                    pool.wait_ge(vsel_ready, 2 * n)
                    normalise(n - 1, q, 0)
                if back:
                    times_e(ways1[q][:, :, :], n + 1, slice(FRONT_WAYS, WAYS)).then_inc(ways1_ready, 1)
                if prev:
                    normalise(n - 1, q, 2)
                    normalise(n - 1, q, 3)
                gather_share(n, 0)
                gather_share(n, 1)
                if front:
                    pool.wait_ge(norm0_ready, n + 3)
                    pool.tensor_tensor(x0, x0, ways0[p][:, V0:V0 + 1, :].to_broadcast([P, F, F]),
                                       ALU.mult).then_inc(weighed0, 1)
                gather_share(n, 2)
                if stages(n + 1)[4]:
                    need(pool, weighed0, n + 2)
                    need(pool, ends_ready, 2 * (n + 2))
                    need(pool, top0_ready, n + 2)
                if prev:
                    normalise(n - 1, q, 4)
                gather_share(n, 3)

            def once(half, turn_no):
                now[0] = half
                if half % 2 and turn_no == 0 and half // 2 + 1 < BLOCKS:
                    pool.wait_ge(emb_ready, ROUNDS * (half // 2 + 2))

            tiles(pool, step, once)

        @block.vector
        def _(dve):
            dve.memset(cw0[PAIRS0 % P:P, TCHUNKS - 1, :], 0.0).then_inc(pads_cleared, 1)
            dve.wait_ge(ident_ready, 1)
            dve.tensor_reduce(group_sel[:, :], ident[:, :].rearrange("p (b k) -> p b k", k=K), X, ALU.add).then_inc(sel_ready, 1)
            dve.tensor_tensor(fold[:, :], ident[:, 0:HALF_ROWS], ident[:, HALF_ROWS:P], ALU.add).then_inc(sel_ready, 1)
            dve.wait_ge(loads_in, LOADS)

            def terms(n, p, c, lo=0, hi=CHUNK_F):
                if lo == 0:
                    need(dve, pooled_done, NP * (n - 2) + FREED[c])
                mid = CHUNK_F - SCALED[c]
                for f in range(c * CHUNK_F + lo, c * CHUNK_F + min(mid, hi)):
                    last = dve.scalar_tensor_tensor(out=x1[p][:, f, :], in0=r1[:, :], scalar=ways1[p][:, A, f:f + 1],
                                                    in1=top1, op0=ALU.mult, op1=ALU.subtract)
                if hi == CHUNK_F:
                    last.then_inc(terms_ready, 1)

            def shift(n, p, c):
                mid, hi = (c + 1) * CHUNK_F - SCALED[c], (c + 1) * CHUNK_F
                dve.wait_ge(scaled_ready, CHUNKS * n + c + 1)
                dve.tensor_tensor(x1[p][:, mid:hi, :], x1[p][:, mid:hi, :],
                                  top1.unsqueeze(1).to_broadcast([P, hi - mid, G1]), ALU.subtract).then_inc(args_ready, 1)

            def normalise(n, q, i):
                part = x1[q][:, PIECES[i]:PIECES[i + 1], :]
                dve.tensor_tensor(part, part, inv1[:, :].unsqueeze(1).to_broadcast([P, PIECES[i + 1] - PIECES[i], G1]),
                                  ALU.mult).then_inc(norm1_ready[i], 1)

            def step(n, p):
                here, prev, done, back, front = stages(n)
                q = 1 - p
                if here:
                    dve.wait_ge(ways1_ready, n + 1)
                    terms(n, p, 0)
                    shift(n, p, 0)
                if prev:
                    dve.wait_ge(exp1_ready, CHUNKS * n)
                    dve.tensor_reduce(part1[:, :], x1[q][:, sum_pe(n - 1):F, :].rearrange("p f g -> p g f"), X,
                                      ALU.add).then_inc(part1_ready, 1)
                if here:
                    terms(n, p, 1)
                    shift(n, p, 1)
                if prev:
                    dve.wait_ge(sum1_done, n)
                    dve.wait_ge(part1_ready, n)
                    dve.tensor_tensor(part1[:, :], sum1[q], part1[:, :], ALU.add).then_inc(total1_ready, 1)
                if front:
                    dve.wait_ge(ways0_ready, n + 3)
                    dve.tensor_reduce(ends[p][:, 0, :], ways0[p][:, A0:A1 + 1, :], X, ALU.max).then_inc(ends_ready, 1)
                    dve.tensor_reduce(ends[p][:, 1, :], ways0[p][:, A0:A1 + 1, :], X, ALU.min).then_inc(ends_ready, 1)
                if prev:
                    dve.wait_ge(total1_ready, n)
                    for i in range(NP):
                        need(dve, norm1_ready[i], n - 1)
                    dve.reciprocal(inv1[:, :], part1[:, :]).then_inc(inv1_ready, 1)
                if front:
                    dve.wait_ge(ends_ready, 2 * (n + 3))
                    dve.tensor_scalar(low0[:, :], ways0[p][:, R0, :], ends[p][:, 1, 0:1], None, ALU.mult).then_inc(low0_ready, 1)
                if prev:
                    dve.wait_ge(inv1_ready, n)
                    normalise(n - 1, q, by_vector(n - 1)[0])
                if front:
                    dve.wait_ge(low0_ready, n + 3)
                    dve.scalar_tensor_tensor(out=top0, in0=ways0[p][:, R0, :], scalar=ends[p][:, 0, 0:1], in1=low0[:, :],
                                             op0=ALU.mult, op1=ALU.max).then_inc(top0_ready, 1)
                if here:
                    terms(n, p, 2, 0, 1)
                if front:
                    dve.wait_ge(top0_ready, n + 3)
                    dve.wait_ge(outer_ready, n + 3)
                    dve.tensor_tensor(x0, x0, top0.unsqueeze(2).to_broadcast([P, F, F]),
                                      ALU.subtract).then_inc(shifted0, 1)
                if here:
                    terms(n, p, 2, 1)
                    shift(n, p, 2)
                if prev:
                    for i in by_vector(n - 1)[1:]:
                        normalise(n - 1, q, i)
                if front:
                    dve.wait_ge(exp0_ready, n + 3)
                    dve.tensor_reduce(sum0[:, :], x0, X, ALU.add).then_inc(sum0_ready, 1)
                if here:
                    terms(n, p, 3, 0, 1)
                if front:
                    dve.wait_ge(sum0_ready, n + 3)
                    dve.reciprocal(rcp0, sum0[:, :]).then_inc(rcp0_ready, 1)
                if here:
                    terms(n, p, 3, 1)
                if front:
                    dve.wait_ge(rcp0_ready, n + 3)
                    dve.tensor_tensor(x0, x0, rcp0.unsqueeze(2).to_broadcast([P, F, F]),
                                      ALU.mult).then_inc(norm0_ready, 1)
                if back:
                    need(dve, terms_ready, CHUNKS * (n + 1))
                    need(dve, scaled_ready, CHUNKS * (n + 1))
                    dve.wait_ge(res_copied, n + 2)
                    dve.tensor_tensor(r1[:, :], res[:, :], wq1[:, :], ALU.mult).then_inc(r1_ready, 1)
                if here:
                    shift(n, p, 3)
                if back:
                    dve.wait_ge(r1_ready, n + 2)
                    dve.tensor_scalar(low1[:, :], r1[:, :], ends[q][:, 1, 1:2], None, ALU.mult).then_inc(low1_ready, 1)
                    dve.wait_ge(low1_ready, n + 2)
                    need(dve, args_ready, CHUNKS * (n + 1))
                    dve.scalar_tensor_tensor(out=top1, in0=r1[:, :], scalar=ends[q][:, 0, 1:2], in1=low1[:, :],
                                             op0=ALU.mult, op1=ALU.max).then_inc(top1_ready, 1)
                if here and sums_half(n):
                    dve.wait_ge(exp1_ready, CHUNKS * n + 3)
                    dve.tensor_reduce(early[:, :], x1[p][:, EARLY_SUM, :].rearrange("p f g -> p g f"), X,
                                      ALU.add).then_inc(early_ready, 1)
                if back:
                    dve.wait_ge(top1_ready, n + 2)

            tiles(dve, step, lambda half, turn_no: None)

        @block.scalar
        def _(act):
            act.wait_ge(loads_in, LOADS)

            def keep_rows(t, r):
                lo, hi = r * ROUND_F, min(F, (r + 1) * ROUND_F)
                act.wait_ge(emb_turned, F * t + hi)
                src = misc[:, 0:(hi - lo) * BLOCK_TILES].rearrange("p (f t) -> p t f", t=BLOCK_TILES)
                base = t % 2 * BLOCK_TILES
                if t == 2:
                    act.copy(emb[:, RING:RING + AHEAD, lo:hi], src[:, 0:AHEAD, :])
                act.copy(emb[:, base:base + BLOCK_TILES, lo:hi], src).then_inc(emb_ready, 1)

            for r in range(ROUNDS):
                keep_rows(0, r)
            now = [0]

            def scale(n, p, c):
                if c == 0:
                    act.wait_ge(r1_ready, n + 1)
                    act.wait_ge(ways1_ready, n + 1)
                need(act, pooled_done, NP * (n - 2) + FREED[c])
                for f in range((c + 1) * CHUNK_F - SCALED[c], (c + 1) * CHUNK_F):
                    last = act.activation(x1[p][:, f, :], r1[:, :], ACT.Copy, scale=ways1[p][:, A, f:f + 1])
                last.then_inc(scaled_ready, 1)

            def exp1(n, p, c):
                act.wait_ge(args_ready, CHUNKS * n + c + 1)
                part = x1[p][:, c * CHUNK_F:(c + 1) * CHUNK_F, :]
                act.activation(part, part, ACT.Exp).then_inc(exp1_ready, 1)

            def keep_turned0(n, g):
                if g == 0:
                    need(act, res_done, n)
                act.wait_ge(turned0, TGROUPS * n + g + 1)
                lo, hi = TGROUP * g, min(TGROUP * (g + 1), TCHUNKS)
                act.copy(x0t[:, lo:hi, :], turn[g % 2][:, 0:(hi - lo) * P].rearrange("p (c q) -> p c q", q=P)
                         ).then_inc(x0t_ready, 1)

            def step(n, p):
                here, prev, done, back, front = stages(n)
                if here:
                    scale(n, p, 1)
                if back:
                    keep_turned0(n + 1, 0)
                    keep_turned0(n + 1, 1)
                if here:
                    exp1(n, p, 0)
                if back:
                    keep_turned0(n + 1, 2)
                    keep_turned0(n + 1, 3)
                if done:
                    act.wait_ge(pooled_done, NP * (n - 1))
                    need(act, pooled_turned, n - 2)
                    act.copy(pooled[:, :, :], pooled_view[:, :, 0:G1]).then_inc(pooled_copied, 1)
                if here:
                    scale(n, p, 2)
                if here:
                    exp1(n, p, 1)
                if front and not sums_half(n):
                    act.wait_ge(shifted0, n + 3)
                    act.activation(x0, x0, ACT.Exp).then_inc(exp0_ready, 1)
                if done:
                    act.wait_ge(pooled_turned, n - 1)
                    if isinstance(n, int):
                        t = (n - 2) % HALF_TILES
                        spot = lambda v: v[:, :, :, t]
                        need(act, z1_done, (n - 2) // HALF_TILES)
                    else:
                        spot = lambda v: v[:, :, :, bass.ds(n - 2 - now[0] * HALF_TILES, 1)].rearrange("p c q o -> p c (q o)")
                        need(act, z1_done, now[0])
                    flat = pooled_t[:, :, :, :, :].rearrange("p c f b t -> p c (f b) t")
                    act.copy(spot(flat[:, :, 0:REGION0_F * GROUPS, :]), pt_ps[:, :, 0, :]).then_inc(pooled_kept, 1)
                    v = spot(flat[:, :, REGION0_F * GROUPS:F * GROUPS, :]).rearrange("p c (j x) -> p c j x", j=4)
                    act.copy(v, pt_ps[:, :, 1, :].rearrange("p c (j x) -> p c j x", j=4)[:, :, :, 0:8]).then_inc(pooled_kept, 1)
                if turns_rows(n):
                    keep_rows(n // (2 * HALF_TILES) + 1, 0)
                if front and sums_half(n):
                    act.wait_ge(shifted0, n + 3)
                    act.activation(x0, x0, ACT.Exp).then_inc(exp0_ready, 1)
                if here:
                    scale(n, p, 3)
                if back:
                    act.wait_ge(res_done, n + 2)
                    need(act, z0_summed, n + 1)
                    need(act, r1_ready, n + 1)
                    act.copy(res[:, :], res_ps).then_inc(res_copied, 1)
                if here:
                    exp1(n, p, 2)
                if turns_rows(n):
                    keep_rows(n // (2 * HALF_TILES) + 1, 1)
                if here:
                    exp1(n, p, 3)
                if back:
                    act.wait_ge(z0_summed, n + 2)
                    act.copy(zt[:, 0:2, bass.ds(GROUPS * (n + 1), GROUPS)], z0_ps).then_inc(z0_kept, 1)
                if turns_rows(n):
                    keep_rows(n // (2 * HALF_TILES) + 1, 2)
                if back:
                    scale(n + 1, 1 - p, 0)

            def once(half, turn_no):
                now[0] = half
                if half and turn_no:
                    act.wait_ge(z1_done, half)
                    need(act, z1_turned, half - 1)
                    act.copy(z1[:, :], misc[:, 0:G1]).then_inc(z1_copied, 1)
                    act.wait_ge(z1_turned, half)
                    dst = zt[:, 2:4, (half - 1) * HALF_ROWS:half * HALF_ROWS].rearrange("p c (t b) -> p c b t", b=GROUPS)
                    for c in range(2):
                        act.copy(dst[:, c], misc[0:HG, 256 + HALF_ROWS * c:256 + HALF_ROWS * (c + 1)]
                                 .rearrange("p (b t) -> p b t", t=HALF_TILES)).then_inc(z1_kept, 1)

            tiles(act, step, once)

            for m in range(H1 // P):
                act.wait_ge(h1_done, m + 1)
                act.activation(h1t[:, m, :], turn[m % 2][:, :], ACT.Relu, bias=b1[:, m:m + 1]).then_inc(h1_ready, 1)
            for m in range(H2 // P):
                act.wait_ge(h2_done, m + 1)
                act.activation(h2t[:, m, :], turn[m % 2][:, :], ACT.Relu, bias=b2[:, m:m + 1]).then_inc(h2_ready, 1)
            act.wait_ge(y_done, 1)
            act.copy(y_sb.rearrange("o (x g t) -> o x t g", g=GROUPS, t=BLOCK_TILES),
                     res_bank[0:1, :].rearrange("o (x t g) -> o x t g", g=GROUPS, t=BLOCK_TILES)).then_inc(y_ready, 1)

        @block.tensor
        def _(pe):
            pe.wait_ge(ident_ready, 1)
            pe.wait_ge(pads_cleared, 2)
            pe.wait_ge(sel_ready, 2)
            pe.wait_ge(loads_in, LOADS)

            def turn_rows(t, r):
                lo, hi = r * ROUND_F, min(F, (r + 1) * ROUND_F)
                pe.wait_ge(rows_in[r], 16 * (hi - lo) * (t + 1))
                need(pe, emb_ready, ROUNDS * t + r)
                if r == 0:
                    need(pe, z1_kept, 2 * (2 * t - 2))
                for f in range(lo, hi):
                    at_f = slice((f - lo) * BLOCK_TILES, (f - lo + 1) * BLOCK_TILES)
                    for g in range(GROUPS):
                        at_g = slice(g * K, (g + 1) * K)
                        last = pe.matmul(misc[at_g, at_f], rows[:, f, :],
                                         ident[:, at_g], start=True, stop=True)
                    last.then_inc(emb_turned, 1)

            for r in range(ROUNDS):
                turn_rows(0, r)

            def sums(n, p, c):
                if sums_half(n) and c in (1, 2):
                    if c == 2:
                        pe.wait_ge(early_ready, n // HALF_TILES)
                        pe.matmul(sum1[p], ident[:, :], early[:, :], start=False, stop=False)
                    return
                pe.wait_ge(exp1_ready, CHUNKS * n + c + 1)
                if c == 0:
                    need(pe, total1_ready, n - 1)
                count = sum_pe(n)
                hi = min(count, (c + 1) * CHUNK_F)
                for f in range(c * CHUNK_F, hi):
                    last = pe.matmul(sum1[p], ident[:, :], x1[p][:, f, :], start=f == 0, stop=f == count - 1)
                if c * CHUNK_F < hi == count:
                    last.then_inc(sum1_done, 1)

            def turn0(n, g):
                if g == 0:
                    pe.wait_ge(weighed0, n + 1)
                need(pe, x0t_ready, TGROUPS * n + g - 1)
                for c in range(TGROUP * g, min(TGROUP * (g + 1), TCHUNKS)):
                    last = pe.transpose(turn[g % 2][:, (c % TGROUP) * P:(c % TGROUP + 1) * P],
                                        x0_pad[:, c * P:(c + 1) * P], ident[:, :])
                last.then_inc(turned0, 1)

            def pool_k(n, q, i):
                if i == 0:
                    pe.wait_ge(vsel_ready, 2 * (n + 1))
                    need(pe, pooled_kept, 2 * n)
                pe.wait_ge(norm1_ready[i], n + 1)
                for f in range(PIECES[i], PIECES[i + 1]):
                    j, region = f % 4, f // REGION0_F
                    row, count = (f - REGION0_F * region) // 4, (REGION0_F, F - REGION0_F)[region] // 4
                    last = pe.matmul(pooled_ps[32 * j:32 * (j + 1), 256 * region:256 * region + G1],
                                     vsel[:, 32 * f:32 * (f + 1)], x1[q][:, f, :],
                                     start=row == 0, stop=row == count - 1)
                last.then_inc(pooled_done, 1)

            Z1_SLOTS = -(-2 * F // 3)
            SLOTS_IN = [(c, slot) for c in range(2) for slot in range(F)]

            def z1_part(half, part):
                lo, hi = part * Z1_SLOTS, min(2 * F, (part + 1) * Z1_SLOTS)
                if lo == 0:
                    pe.wait_ge(cw1_in, 32)
                    pe.wait_ge(pooled_kept, 2 * HALF_TILES * half)
                    need(pe, z1_kept, 2 * (half - 1))
                    pe.wait_ge(emb_ready, ROUNDS * min(BLOCKS, 1 + (half + 1) // 2))
                flat = pooled_t[:, :, :, :, :].rearrange("p c f b t -> p c f (b t)")
                for c, slot in SLOTS_IN[lo:hi]:
                    if slot < REGION0_F:
                        f = slot // 8 + 4 * (slot % 8)
                    else:
                        f = REGION0_F + (slot - REGION0_F) // 2 + 4 * (slot % 2)
                    side = slot % 2
                    last = pe.matmul(misc[HALF_ROWS * side:HALF_ROWS * (side + 1), 0:G1], flat[:, c, slot, :],
                                     cw1[:, c, f, :], start=c == 0 and slot < 2, stop=c == 1 and slot >= F - 2)
                if hi == 2 * F:
                    last.then_inc(z1_done, 1)

            def step(n, p):
                here, prev, done, back, front = stages(n)
                q = 1 - p
                if back:
                    turn0(n + 1, 0)
                    turn0(n + 1, 1)
                if prev:
                    sums(n - 1, q, 3)
                if back:
                    turn0(n + 1, 2)
                    turn0(n + 1, 3)
                if done:
                    pool_k(n - 2, p, 4)
                if back:
                    need(pe, z0_kept, n + 1)
                    for c in range(TCHUNKS):
                        if c % TGROUP == 0:
                            pe.wait_ge(x0t_ready, TGROUPS * (n + 1) + c // TGROUP + 1)
                        last = pe.matmul(res_ps, x0t[:, c, :], cw0[:, c, :], start=c == 0, stop=c == TCHUNKS - 1)
                    last.then_inc(res_done, 1)
                if here:
                    sums(n, p, 0)
                if done:
                    pe.wait_ge(pooled_copied, n - 1)
                    for c in range(2):
                        for r in range(2):
                            last = pe.transpose(pt_ps[:, c, r, :], pooled[:, r, c * HG:(c + 1) * HG], ident[:, :])
                    last.then_inc(pooled_turned, 1)
                if sums_half(n):
                    z1_part(n // HALF_TILES, 0)
                if turns_rows(n):
                    turn_rows(n // (2 * HALF_TILES) + 1, 0)
                if here:
                    sums(n, p, 1)
                if prev:
                    pool_k(n - 1, q, 0)
                    pool_k(n - 1, q, 1)
                    pool_k(n - 1, q, 2)
                if turns_rows(n):
                    turn_rows(n // (2 * HALF_TILES) + 1, 1)
                if back:
                    pe.wait_ge(res_copied, n + 2)
                    for c in range(2):
                        last = pe.matmul(z0_ps[:, c, :], res[:, c * HG:(c + 1) * HG], group_sel[:, :], start=True, stop=True)
                    last.then_inc(z0_summed, 1)
                if sums_half(n):
                    z1_part(n // HALF_TILES, 1)
                if here:
                    sums(n, p, 2)
                if sums_half(n):
                    z1_part(n // HALF_TILES, 2)
                if prev:
                    pool_k(n - 1, q, 3)
                if turns_rows(n):
                    turn_rows(n // (2 * HALF_TILES) + 1, 2)

            def z1_fold(half):
                pe.wait_ge(z1_copied, half)
                for c in range(2):
                    last = pe.matmul(misc[0:HG, 256 + HALF_ROWS * c:256 + HALF_ROWS * (c + 1)],
                                     z1[:, c * HG:(c + 1) * HG], fold[:, :], start=True, stop=True)
                last.then_inc(z1_turned, 1)

            def once(half, turn_no):
                if half and turn_no:
                    z1_fold(half)

            tiles(pe, step, once)

            pe.wait_ge(mlp_in, 64)
            pe.wait_ge(z1_kept, 2 * HALVES)
            pe.wait_ge(z0_kept, TILES)
            for m in range(H1 // P):
                need(pe, h1_ready, m - 1)
                cols = slice(m * P, (m + 1) * P)
                for c in range(4):
                    pe.matmul(turn[m % 2][:, :], w1[:, c, cols], zt[:, c, :], start=c == 0, stop=False)
                pe.matmul(turn[m % 2][:, :], w1d[:, cols], dense_t, start=False, stop=True).then_inc(h1_done, 1)
            pe.wait_ge(h1_ready, H1 // P)
            for m in range(H2 // P):
                for c in range(H1 // P):
                    last = pe.matmul(turn[m % 2][:, :], w2[:, c, m * P:(m + 1) * P], h1t[:, c, :],
                                     start=c == 0, stop=c == H1 // P - 1)
                last.then_inc(h2_done, 1)
            pe.wait_ge(h2_ready, H2 // P)
            for c in range(H2 // P):
                last = pe.matmul(res_bank[0:1, :], w3[:, c:c + 1], h2t[:, c, :], start=c == 0, stop=c == H2 // P - 1)
            last.then_inc(y_done, 1)


def kernel(**inputs):
    import numpy as np
    import concourse.bacc as bacc
    from concourse import mybir
    from concourse.bass_utils import run_bass_kernel_spmd

    a = {k: np.asarray(v) for k, v in inputs.items()}
    by_k = lambda name: a[name][0].T
    laid = {
        "ids": a["ids"],
        "field_w": np.stack([by_k(f"L0_rec_{w}") for w in ("wk0", "wk1", "wq0", "wv0", "wk1", "wv1")], axis=1),
        "wq1": by_k("L0_rec_wq1"),
        "cw0": a["L0_rec_cw0"][0].reshape(F, F, G1).transpose(1, 0, 2).reshape(PAIRS0, G1),
        "cw1": a["L0_rec_cw1"][0].reshape(F, 2, HG, G1).transpose(2, 1, 0, 3),
        "dense_t": a["dense_ctx"].reshape(BLOCKS, GROUPS, BLOCK_TILES, DENSE).transpose(3, 0, 2, 1).reshape(DENSE, B),
        "w1": a["W_top1"],
        "b1": a["b_top1"].reshape(H1 // P, P).T,
        "w2": a["W_top2"],
        "b2": a["b_top2"].reshape(H2 // P, P).T,
        "w3": a["W_top3"].reshape(H2 // P, P).T,
    }
    for f in range(F):
        laid[f"tbl_{f}"] = a[f"tbl_{f}"]
    laid = {k: np.ascontiguousarray(v) for k, v in laid.items()}

    nc = bacc.Bacc("TRN2", target_bir_lowering=False, num_devices=1)
    dram = {k: nc.dram_tensor(f"in_{k}", v.shape, mybir.dt.from_np(v.dtype), kind="ExternalInput").ap() for k, v in laid.items()}
    out = nc.dram_tensor("out", (B, 1), mybir.dt.float32, kind="ExternalOutput").ap()
    build(nc, dram, out.rearrange("b o -> o b"))
    r = run_bass_kernel_spmd(nc, [{f"in_{k}": v for k, v in laid.items()}], core_ids=[0])
    return r.results[0]["out"]
```
